# Optimizing a Trainium2 kernel written in Bass

```python
import numpy as np
import jax
import jax.numpy as jnp

def _softmax(x, axis=-1):
    return jax.nn.softmax(x, axis=axis)

def _gelu(x):
    return jax.nn.gelu(x, approximate=True)

def _silu(x):
    return jax.nn.silu(x)

def _sigmoid(x):
    return jax.nn.sigmoid(x)

def _layernorm(x, axis=-1, eps=1e-05):
    m = jnp.mean(x, axis=axis, keepdims=True)
    v = jnp.var(x, axis=axis, keepdims=True)
    return (x - m) / jnp.sqrt(v + eps)

def _scatter_add(tgt, idx, src, axis=0):
    return tgt.at[idx].add(src)

def _segment_sum(src, seg, n):
    return jax.ops.segment_sum(src, seg, n)
kernel_name = 'mk_adaln_d1_jaxref_r4_c004ab'

def setup_inputs(seed: int=0):
    np.random.seed(seed)
    _w = jnp.asarray

    def _L0_attn_setup():
        import jax, jax.numpy as jnp
        import numpy as np
        HIDDEN = 256
        STATE = 16
        EXPAND = 2
        INNER = HIDDEN * EXPAND
        BATCH, SEQ = (4, 512)
        key = jax.random.key(seed)
        ks = jax.random.split(key, 12)
        s = 0.02
        return {'x': jax.random.normal(ks[0], (BATCH, SEQ, HIDDEN), jnp.float32), 'norm_scale': jnp.ones((HIDDEN,), jnp.float32), 'norm_bias': jnp.zeros((HIDDEN,), jnp.float32), 'W_in': jax.random.normal(ks[1], (HIDDEN, 2 * INNER), jnp.float32) * s, 'conv_w': jax.random.normal(ks[2], (INNER, 3), jnp.float32) * 0.3, 'conv_b': jnp.zeros((INNER,), jnp.float32), 'W_dt': jax.random.normal(ks[3], (INNER, INNER), jnp.float32) * s, 'b_dt': jnp.zeros((INNER,), jnp.float32), 'A_log': jax.random.normal(ks[4], (INNER, STATE), jnp.float32), 'D_param': jnp.ones((INNER,), jnp.float32), 'W_B': jax.random.normal(ks[5], (INNER, STATE), jnp.float32) * s, 'W_C': jax.random.normal(ks[6], (INNER, STATE), jnp.float32) * s, 'W_out': jax.random.normal(ks[7], (INNER, HIDDEN), jnp.float32) * s}
    _L0_attn_in = _L0_attn_setup()

    def _L0_ffn_setup():
        import jax, jax.numpy as jnp
        import numpy as np
        TOP_K = 4
        N_GROUP = 4
        TOPK_GROUP = 2
        ROUTED_SCALING = 1.0

        def _route(x_flat, gate_weight, e_bias):
            T = x_flat.shape[0]
            E = gate_weight.shape[0]
            logits = jnp.einsum('th,eh->te', x_flat, gate_weight)
            scores = jax.nn.sigmoid(logits)
            scores_for_choice = scores + e_bias[None, :]
            grp = scores_for_choice.reshape(T, N_GROUP, E // N_GROUP)
            top2, _ = jax.lax.top_k(grp, 2)
            group_scores = top2.sum(axis=-1)
            _, group_idx = jax.lax.top_k(group_scores, TOPK_GROUP)
            group_mask = jax.nn.one_hot(group_idx, N_GROUP, dtype=scores.dtype).sum(axis=1)
            score_mask = jnp.repeat(group_mask, E // N_GROUP, axis=1)
            tmp_scores = jnp.where(score_mask > 0, scores_for_choice, 0.0)
            _, topk_idx = jax.lax.top_k(tmp_scores, TOP_K)
            topk_weight = jnp.take_along_axis(scores, topk_idx, axis=1)
            denom = topk_weight.sum(axis=-1, keepdims=True) + 1e-20
            topk_weight = topk_weight / denom * ROUTED_SCALING
            return (topk_idx, topk_weight)
        key = jax.random.key(seed)
        k1, k2, k3, k4, k5 = jax.random.split(key, 5)
        B, S, H, I, E = (1, 512, 256, 128, 16)
        hidden_states = jax.random.normal(k1, (B, S, H), dtype=jnp.float32)
        gate_weight = jax.random.normal(k2, (E, H), dtype=jnp.float32) * (1.0 / np.sqrt(H))
        e_bias = jnp.zeros((E,), dtype=jnp.float32)
        gate_proj = jax.random.normal(k3, (E, I, H), dtype=jnp.float32) * 0.02
        up_proj = jax.random.normal(k4, (E, I, H), dtype=jnp.float32) * 0.02
        down_proj = jax.random.normal(k5, (E, H, I), dtype=jnp.float32) * 0.02
        return {'hidden_states': hidden_states, 'gate_weight': gate_weight, 'e_bias': e_bias, 'gate_proj': gate_proj, 'up_proj': up_proj, 'down_proj': down_proj}
    _L0_ffn_in = _L0_ffn_setup()
    _L0_c = _w((lambda *s: np.random.randn(*s).astype(np.float32) * 0.05)(16, 256))
    _L0_wmod = _w((lambda *s: np.random.randn(*s).astype(np.float32) * 0.05)(256, 6 * 256) * 256 ** (-0.5))
    _d = {'L0_attn_x': _L0_attn_in['x'], 'L0_attn_norm_scale': _L0_attn_in['norm_scale'], 'L0_attn_norm_bias': _L0_attn_in['norm_bias'], 'L0_attn_W_in': _L0_attn_in['W_in'], 'L0_attn_conv_w': _L0_attn_in['conv_w'], 'L0_attn_conv_b': _L0_attn_in['conv_b'], 'L0_attn_W_dt': _L0_attn_in['W_dt'], 'L0_attn_b_dt': _L0_attn_in['b_dt'], 'L0_attn_A_log': _L0_attn_in['A_log'], 'L0_attn_D_param': _L0_attn_in['D_param'], 'L0_attn_W_B': _L0_attn_in['W_B'], 'L0_attn_W_C': _L0_attn_in['W_C'], 'L0_attn_W_out': _L0_attn_in['W_out'], 'L0_ffn_gate_weight': _L0_ffn_in['gate_weight'], 'L0_ffn_e_bias': _L0_ffn_in['e_bias'], 'L0_ffn_gate_proj': _L0_ffn_in['gate_proj'], 'L0_ffn_up_proj': _L0_ffn_in['up_proj'], 'L0_ffn_down_proj': _L0_ffn_in['down_proj'], 'L0_c': _L0_c, 'L0_wmod': _L0_wmod}
    _x0 = _d['L0_attn_x']
    _d['L0_attn_x'] = jax.random.normal(jax.random.fold_in(jax.random.key(seed), 1), (16, 512, 256), dtype=_x0.dtype)
    del _x0
    return _d

def reference(L0_attn_x, L0_attn_norm_scale, L0_attn_norm_bias, L0_attn_W_in, L0_attn_conv_w, L0_attn_conv_b, L0_attn_W_dt, L0_attn_b_dt, L0_attn_A_log, L0_attn_D_param, L0_attn_W_B, L0_attn_W_C, L0_attn_W_out, L0_ffn_gate_weight, L0_ffn_e_bias, L0_ffn_gate_proj, L0_ffn_up_proj, L0_ffn_down_proj, L0_c, L0_wmod):

    def _L0_attn_ref(x, norm_scale, norm_bias, W_in, conv_w, conv_b, W_dt, b_dt, A_log, D_param, W_B, W_C, W_out):
        import jax, jax.numpy as jnp
        import numpy as np
        HIDDEN = 256
        STATE = 16
        EXPAND = 2
        INNER = HIDDEN * EXPAND
        BATCH, SEQ = (4, 512)
        residual = x
        mu = jnp.mean(x, axis=-1, keepdims=True)
        var = jnp.mean(jnp.square(x - mu), axis=-1, keepdims=True)
        xn = (x - mu) * jax.lax.rsqrt(var + 1e-05) * norm_scale + norm_bias
        xz = xn @ W_in
        xb, z = jnp.split(xz, 2, axis=-1)
        xp = jnp.pad(xb, ((0, 0), (1, 1), (0, 0)))
        xb = conv_w[:, 0] * xp[:, :-2] + conv_w[:, 1] * xp[:, 1:-1] + conv_w[:, 2] * xp[:, 2:] + conv_b
        xb = jax.nn.silu(xb)
        dt = jax.nn.softplus(xb @ W_dt + b_dt)
        A = -jnp.exp(A_log)
        Bi = xb @ W_B
        Ci = xb @ W_C

        def step(h, inp):
            x_t, dt_t, B_t, C_t = inp
            A_bar = jnp.exp(dt_t[:, :, None] * A)
            h = A_bar * h + (dt_t * x_t)[:, :, None] * B_t[:, None, :]
            y_t = jnp.einsum('bdn,bn->bd', h, C_t)
            return (h, y_t)
        h0 = jnp.zeros((x.shape[0], INNER, STATE), x.dtype)
        xs = (jnp.swapaxes(xb, 0, 1), jnp.swapaxes(dt, 0, 1), jnp.swapaxes(Bi, 0, 1), jnp.swapaxes(Ci, 0, 1))
        _, y = jax.lax.scan(step, h0, xs)
        y = jnp.swapaxes(y, 0, 1)
        y = (y + D_param * xb) * jax.nn.silu(z)
        return residual + y @ W_out

    def _L0_ffn_ref(hidden_states, gate_weight, e_bias, gate_proj, up_proj, down_proj):
        import jax, jax.numpy as jnp
        import numpy as np
        TOP_K = 4
        N_GROUP = 4
        TOPK_GROUP = 2
        ROUTED_SCALING = 1.0

        def _route(x_flat, gate_weight, e_bias):
            T = x_flat.shape[0]
            E = gate_weight.shape[0]
            logits = jnp.einsum('th,eh->te', x_flat, gate_weight)
            scores = jax.nn.sigmoid(logits)
            scores_for_choice = scores + e_bias[None, :]
            grp = scores_for_choice.reshape(T, N_GROUP, E // N_GROUP)
            top2, _ = jax.lax.top_k(grp, 2)
            group_scores = top2.sum(axis=-1)
            _, group_idx = jax.lax.top_k(group_scores, TOPK_GROUP)
            group_mask = jax.nn.one_hot(group_idx, N_GROUP, dtype=scores.dtype).sum(axis=1)
            score_mask = jnp.repeat(group_mask, E // N_GROUP, axis=1)
            tmp_scores = jnp.where(score_mask > 0, scores_for_choice, 0.0)
            _, topk_idx = jax.lax.top_k(tmp_scores, TOP_K)
            topk_weight = jnp.take_along_axis(scores, topk_idx, axis=1)
            denom = topk_weight.sum(axis=-1, keepdims=True) + 1e-20
            topk_weight = topk_weight / denom * ROUTED_SCALING
            return (topk_idx, topk_weight)
        B, S, H = hidden_states.shape
        E = gate_proj.shape[0]
        x = hidden_states.reshape(-1, H).astype(jnp.float32)
        topk_idx, topk_weight = _route(x, gate_weight, e_bias)
        combine = (jax.nn.one_hot(topk_idx, E, dtype=x.dtype) * topk_weight[..., None]).sum(axis=1)
        g = jnp.einsum('th,eih->tei', x, gate_proj)
        u = jnp.einsum('th,eih->tei', x, up_proj)
        act = jax.nn.silu(g) * u
        expert_out = jnp.einsum('tei,ehi->teh', act, down_proj)
        y = jnp.einsum('teh,te->th', expert_out, combine)
        return y.reshape(B, S, H)
    x = L0_attn_x
    mod = (_silu(L0_c) @ L0_wmod).reshape(L0_c.shape[0], 6, 1, -1)
    sa, ca, ga, sb, cb, gb = (mod[:, 0], mod[:, 1], mod[:, 2], mod[:, 3], mod[:, 4], mod[:, 5])
    ga = (2 * (ga >= 0) - 1) * jnp.maximum(jnp.abs(ga), 0.25)
    gb = (2 * (gb >= 0) - 1) * jnp.maximum(jnp.abs(gb), 0.25)
    h = _layernorm(x, axis=-1) * (1 + ca) + sa
    x = x + ga * _L0_attn_ref(h, L0_attn_norm_scale, L0_attn_norm_bias, L0_attn_W_in, L0_attn_conv_w, L0_attn_conv_b, L0_attn_W_dt, L0_attn_b_dt, L0_attn_A_log, L0_attn_D_param, L0_attn_W_B, L0_attn_W_C, L0_attn_W_out)
    h = _layernorm(x, axis=-1) * (1 + cb) + sb
    x = x + gb * _L0_ffn_ref(h, L0_ffn_gate_weight, L0_ffn_e_bias, L0_ffn_gate_proj, L0_ffn_up_proj, L0_ffn_down_proj)
    return x

_drawn_inputs = setup_inputs


def setup_inputs(seed=0):
    import zlib

    import numpy as np

    out = dict(_drawn_inputs(seed))
    spreads = {'L0_attn_norm_scale': (1.0, 0.2),
     'L0_attn_norm_bias': (0.0, 0.1),
     'L0_attn_conv_b': (0.0, 0.1),
     'L0_attn_b_dt': (0.0, 0.1),
     'L0_attn_D_param': (1.0, 0.2),
     'L0_ffn_e_bias': (0.0, 0.1)}
    factors = {}
    for name, (base, spread) in spreads.items():
        noise = np.random.default_rng([zlib.crc32(name.encode()), seed]).standard_normal(out[name].shape)
        drawn = base * np.exp(spread * noise) if base else spread * noise
        out[name] = jnp.asarray(drawn.astype(out[name].dtype))
    for name, factor in factors.items():
        out[name] = (out[name] * factor).astype(out[name].dtype)
    return out
```

```python
from contextlib import ExitStack

import concourse.bass as bass
from concourse import mybir

F32 = mybir.dt.float32
BF16 = mybir.dt.bfloat16
ALU = mybir.AluOpType
ACT = mybir.ActivationFunctionType
AX = mybir.AxisListType

P = 128
ENGINES = ("tensor", "vector", "scalar", "gpsimd", "sync")


class Token:

    def __init__(self, engine, part, sem, step):
        self.engine, self.part, self.sem, self.step = engine, part, sem, step
        self.waited = False
        self.count = 0


class Program:

    def __init__(self, nc, sems, dma_sems):
        self.nc, self.sems, self.dma_sems = nc, sems, dma_sems
        self.parts = []

    def begin(self, loop=None):
        self.parts.append({"loop": loop, "queue": {e: [] for e in ENGINES}, "tokens": []})

    def op(self, engine, emit, after=()):
        part = self.parts[-1]
        tok = Token(engine, len(self.parts) - 1, self.sems[engine], 1)
        self._queue(part, engine, emit, after, tok)
        return tok

    def before(self, *names):
        return [Token(n, -1, self.sems.get(n) or self.dma_sems[n], 1) for n in names]

    def dma(self, engine, stream, emit, after=()):
        part = self.parts[-1]
        tok = Token(engine, len(self.parts) - 1, self.dma_sems[stream], 16)
        tok.waited = True
        self._queue(part, engine, emit, after, tok)
        return tok

    def _queue(self, part, engine, emit, after, tok):
        after = flat(after)
        part["queue"][engine].append((emit, after, tok))
        part["tokens"].append(tok)
        for t in after:
            t.waited = True

    def close(self):
        totals = {}
        for part in self.parts:
            last = {}
            for t in part["tokens"]:
                last[t.sem] = t
            for t in last.values():
                t.waited = True
            local = {}
            for t in part["tokens"]:
                if t.waited:
                    local[t.sem] = local.get(t.sem, 0) + t.step
                    t.count = local[t.sem]
            part["base"] = dict(totals)
            part["per_turn"] = local
            turns = 1 if part["loop"] is None else part["loop"][1] - part["loop"][0]
            for s, n in local.items():
                totals[s] = totals.get(s, 0) + n * turns
        self.totals = totals

    def replay(self, eng, engine):
        for index, part in enumerate(self.parts):
            if part["loop"] is None:
                self._run(eng, engine, index, part, None)
            elif part["queue"][engine]:
                with eng.Fori(*part["loop"]) as i:
                    self._run(eng, engine, index, part, i)

    def _run(self, eng, engine, index, part, i):
        seen = {}
        for emit, after, tok in part["queue"][engine]:
            need = {}
            for t in after:
                local = t.count if t.part == index else 0
                need[t.sem] = max(need.get(t.sem, 0), local)
            for sem, local in need.items():
                if seen.get(sem, -1) >= local:
                    continue
                seen[sem] = local
                value = part["base"].get(sem, 0) + local
                if part["loop"] is not None:
                    assert value > 0, (engine, sem)
                    per, first = part["per_turn"].get(sem, 0), part["loop"][0]
                    eng.wait_ge(sem, i * per + (value - first * per))
                elif value:
                    eng.wait_ge(sem, value)
            made = emit(eng, i)
            if tok.waited:
                made.then_inc(tok.sem, tok.step)


def flat(tokens):
    if isinstance(tokens, Token):
        return [tokens]
    return [t for x in tokens or () for t in flat(x)]


def interleave(*streams):
    done = [0] * len(streams)
    live = list(range(len(streams)))
    while live:
        k = min(live, key=lambda s: (done[s] + 1) / streams[s][1])
        try:
            next(streams[k][0])
            done[k] += 1
        except StopIteration:
            live.remove(k)


def build(nc, d, out):
    NB, T, H = d["L0_attn_x"].shape
    INNER = d["L0_attn_W_dt"].shape[0]
    NS = d["L0_attn_A_log"].shape[1]
    E, I, _ = d["L0_ffn_gate_proj"].shape
    NMOD = 6
    TT, HK, DK = T // P, H // P, INNER // P
    BC = 2 * NS
    SPLIT = 3
    NGRP, GRP = 4, E // 4
    EPS = 1e-5
    NEG = -3.0e38
    NU = 2 * NS
    RING, B_RING, C_RING, MOE_RING = 8, 2, 4, 3
    EXPERTS_FROM = 10
    HT = T // 2
    FULL = P // 4
    assert BC == FULL and I == P and E <= FULL and DK == 4 and TT * H == 2 * T

    ctx = ExitStack()
    with ctx:
        def sb(name, shape, dt=F32):
            return ctx.enter_context(nc.sbuf_tensor(name, shape, dt))

        w_in = sb("w_in", [P, HK, 2 * INNER])
        w_dt = sb("w_dt", [P, DK, INNER])
        w_bc = sb("w_bc", [P, DK, SPLIT * BC])
        w_out = sb("w_out", [P, DK, H])
        gate_t = sb("gate_t", [P, E, HK, I])
        up_t = sb("up_t", [P, E, HK, I])
        down_t = sb("down_t", [I, E, H])
        router_t = sb("router_t", [P, HK, E])
        ident = sb("ident", [P, P])
        sel = sb("sel", [SPLIT * FULL, BC], BF16)
        conv_w = sb("conv_w", [P, DK, 3])
        conv_b = sb("conv_b", [P, DK])
        b_dt = sb("b_dt", [P, DK])
        d_par = sb("d_par", [P, DK])
        a_neg = sb("a_neg", [P, DK, NS])
        n_scale = sb("n_scale", [P, HK])
        n_bias = sb("n_bias", [P, HK])
        e_bias = sb("e_bias", [P, E])
        lower = sb("lower", [P, NGRP, NGRP])
        minus_half = sb("minus_half", [P, TT])
        xt = sb("xt", [P, TT, H])
        ht = sb("ht", [P, TT, H])
        x1 = sb("x1", [P, TT, H])
        h2_t = sb("h2_t", [P, HK, T])
        base = sb("base", [P, TT, H])
        xn_t = sb("xn_t", [P, HK, T])
        mod_row = sb("mod_row", [P, 2, H])
        ga_row = sb("ga_row", [P, H])
        gb_row = sb("gb_row", [P, H])
        mod_col = sb("mod_col", [P, 2 * HK])
        xb = sb("xb", [P, DK, T])
        gz = sb("gz", [P, DK, T])
        dt = sb("dt", [P, DK, T])
        dtx = sb("dtx", [P, DK, T])
        unit = sb("unit", [P, RING, 2, T])
        decays = sb("decays", [P, 2, T])
        b_bc = sb("b_bc", [P, B_RING, T])
        c_bc = sb("c_bc", [P, C_RING, T])
        conv = sb("conv", [P, 2, T])
        z2 = sb("z2", [P, TT, H])
        diag_d = sb("diag_d", [P, DK, P])
        bc_stack = sb("bc_stack", [SPLIT * FULL, T], BF16)
        bc_next = sb("bc_next", [SPLIT * FULL, T], BF16)
        w_stack = sb("w_stack", [SPLIT * FULL, T], BF16)
        rest = conv[0:SPLIT * FULL, 0, :]
        second = sb("second", [SPLIT * FULL, T], BF16)
        act = sb("act", [P, MOE_RING, HT])
        etanh = sb("etanh", [P, 2, HT])
        w_all = sb("w_all", [P, 2, HT])
        st = sb("st", [P, TT, 6])
        mv = sb("mv", [P, TT, 2])
        ve = sb("ve", [P, TT])
        rstd = sb("rstd", [P, TT])
        st2 = sb("st2", [P, TT, 6])
        mv2 = sb("mv2", [P, TT, 2])
        ve2 = sb("ve2", [P, TT])
        rstd2 = sb("rstd2", [P, TT])
        mark = sb("mark", [P, 1])
        r_th = sb("r_th", [P, TT, E])
        r_s = sb("r_s", [P, TT, E])
        r_ch = sb("r_ch", [P, TT, E])
        r_hi = sb("r_hi", [P, TT * NGRP, 2])
        r_lo = sb("r_lo", [P, TT * NGRP, 2])
        r_top = sb("r_top", [P, TT * NGRP])
        r_m2 = sb("r_m2", [P, TT * NGRP])
        r_m3 = sb("r_m3", [P, TT * NGRP])
        r_g = sb("r_g", [P, TT * NGRP])
        r_gt = sb("r_gt", [P, TT, NGRP, NGRP])
        r_eq = sb("r_eq", [P, TT, NGRP, NGRP])
        r_cnt = sb("r_cnt", [P, TT * NGRP])
        r_msk = sb("r_msk", [P, TT * NGRP])
        r_tmp = sb("r_tmp", [P, TT, E + 4])
        r_m8 = sb("r_m8", [P, TT, 8])
        r_cut = sb("r_cut", [P, TT, E + 4])
        r_sel = sb("r_sel", [P, TT, E])
        r_w = sb("r_w", [P, TT, E])
        r_den = sb("r_den", [P, TT])
        r_rec = sb("r_rec", [P, TT])
        w3 = sb("w3", [P, TT, SPLIT * FULL])

        ring = unit[:, :, :, :].rearrange("p r a t -> p (r a t)")
        wmod = ring[:, 0:2 * NMOD * H].rearrange("p (k n) -> p k n", k=2)
        stage = [ring[:, q * 4 * H:(q + 1) * 4 * H] for q in range(3, 6)]
        c_t = dtx[:, 0, 0:2 * NB].rearrange("p (k b) -> p k b", k=2)
        c_th = dtx[:, 0, 64:64 + 2 * NB].rearrange("p (k b) -> p k b", k=2)
        c_si = dtx[:, 0, 128:128 + 2 * NB].rearrange("p (k b) -> p k b", k=2)
        modr = dt[0:NB, :, :].rearrange("p a t -> p (a t)")
        gabs = gz[0:NB, 0, 0:H]
        gsgn = gz[0:NB, 1, 0:H]

        ybank = ctx.enter_context(nc.psum_tensor("ybank", [P, 2, T], F32))
        mbank = ctx.enter_context(nc.psum_tensor("mbank", [P, T], F32))
        wbank = [ctx.enter_context(nc.psum_tensor(f"wbank{k}", [P, T], F32)) for k in range(5)]

        mod_dram = nc.dram_tensor("mod_scratch", (NB, NMOD * H), F32, kind="Internal").ap()

        sems = {e: ctx.enter_context(nc.semaphore(f"done_{e}")) for e in ENGINES}
        dma_sems = {s: ctx.enter_context(nc.semaphore(f"dma_{s}")) for s in
                    ("weights", "stage0", "stage1", "stage2", "x", "mods", "ga", "gb", "cols", "out")}
        pr = Program(nc, sems, dma_sems)

        def pe(emit, *after):
            return pr.op("tensor", emit, after)

        def ve_(emit, *after):
            return pr.op("vector", emit, after)

        def pause(*after):
            ve_(lambda e, i: e.memset(mark[:, :], 0.0), *after)

        def sc(emit, *after):
            return pr.op("scalar", emit, after)

        def po(emit, *after):
            return pr.op("gpsimd", emit, after)

        last = {}

        rings = {"work": [0, 1, 2], "experts": [3, 4]}
        work = {"free": [None] * 5, "k": 0}

        def fill(matmuls, *after, ring="work"):
            k = next(b for b in rings[ring] if work["free"][b] != "held")
            rings[ring] = [b for b in rings[ring] if b != k] + [k]
            work["k"] = k
            tok = None
            for n, m in enumerate(matmuls):
                waits = (*after, work["free"][k]) if n == 0 else ()
                tok = pe(lambda e, i, m=m, b=wbank[k]: m(e, i, b), *waits)
            work["free"][k] = "held"
            return wbank[k], tok

        def freed(tok, bank=None):
            k = work["k"] if bank is None else next(n for n, b in enumerate(wbank) if b is bank)
            work["free"][k] = tok
            return tok

        def setup():
            loads = []

            def load(dst, src):
                loads.append(pr.dma("sync", "weights", lambda e, i: e.dma_start(dst, src)))

            for k in range(2):
                load(c_t[:, k, :], d["L0_c"][:, k * P:(k + 1) * P].rearrange("b p -> p b"))
            load(wmod, d["L0_wmod"].rearrange("(k p) n -> p k n", p=P))
            load(w_in[:, :, :], d["L0_attn_W_in"].rearrange("(k p) n -> p k n", p=P))
            load(w_dt[:, :, :], d["L0_attn_W_dt"].rearrange("(k p) n -> p k n", p=P))
            for s in range(SPLIT):
                load(w_bc[:, :, s * BC:s * BC + NS], d["L0_attn_W_B"].rearrange("(k p) n -> p k n", p=P))
                load(w_bc[:, :, s * BC + NS:(s + 1) * BC], d["L0_attn_W_C"].rearrange("(k p) n -> p k n", p=P))
            load(w_out[:, :, :], d["L0_attn_W_out"].rearrange("(k p) n -> p k n", p=P))
            for k in range(HK):
                load(router_t[:, k, :], d["L0_ffn_gate_weight"][:, k * P:(k + 1) * P].rearrange("e p -> p e"))
            load(conv_w[:, :, :], d["L0_attn_conv_w"].rearrange("(k p) n -> p k n", p=P))
            load(a_neg[:, :, :], d["L0_attn_A_log"].rearrange("(k p) n -> p k n", p=P))
            for dst, src in ((conv_b, "conv_b"), (b_dt, "b_dt"), (d_par, "D_param"),
                             (n_scale, "norm_scale"), (n_bias, "norm_bias")):
                load(dst[:, :], d["L0_attn_" + src].rearrange("(k p) -> p k", p=P))
            load(e_bias[:, :], d["L0_ffn_e_bias"].rearrange("(a e) -> a e", a=1).to_broadcast([P, E]))
            weights = loads[-1]

            t = po(lambda e, i: e.memset(ident[:, :], 0.0))
            last["ident"] = po(lambda e, i: e.affine_select(
                out=ident[:, :], in_=ident[:, :], compare_op=ALU.not_equal, fill=1.0, base=0,
                pattern=[[-1, P]], channel_multiplier=1), t)
            t = po(lambda e, i: e.memset(sel[:, :], 0.0))
            for s in range(SPLIT):
                t = po(lambda e, i, s=s: e.affine_select(
                    out=sel[:, :], in_=sel[:, :], compare_op=ALU.not_equal, fill=1.0, base=-s * FULL,
                    pattern=[[-1, BC]], channel_multiplier=1), t)
            last["sel"] = t
            t = po(lambda e, i: e.memset(lower[:, :, :], 1.0))
            t = po(lambda e, i: e.affine_select(
                out=lower[:, :, :], in_=lower[:, :, :], compare_op=ALU.is_gt, fill=0.0, base=0,
                pattern=[[1, NGRP], [-1, NGRP]], channel_multiplier=0), t)
            t = po(lambda e, i: e.memset(minus_half[:, :], -0.5))
            po(lambda e, i: e.memset(w3[:, :, :], 0.0))
            last["const"] = po(lambda e, i: e.memset(r_tmp[:, :, E:], NEG))

            ve_(lambda e, i: e.tensor_scalar(conv_w[:, :, :], conv_w[:, :, :], 0.5, None, ALU.mult), weights)
            ve_(lambda e, i: e.tensor_scalar(conv_b[:, :], conv_b[:, :], 0.5, None, ALU.mult))
            ve_(lambda e, i: e.tensor_scalar(w_out[:, :, :], w_out[:, :, :], 0.5, None, ALU.mult))
            for m_ in range(DK):
                last["diag"] = ve_(lambda e, i, m_=m_: e.tensor_scalar(
                    diag_d[:, m_, :], ident[:, :], d_par[:, m_:m_ + 1], None, ALU.mult), last["ident"])
            t = sc(lambda e, i: e.activation(a_neg[:, :, :], a_neg[:, :, :], ACT.Exp), weights)
            last["halved"] = ve_(lambda e, i: e.tensor_scalar(a_neg[:, :, :], a_neg[:, :, :], -1.0, None, ALU.mult), t)

            t = sc(lambda e, i: e.activation(c_th, c_t, ACT.Tanh, scale=0.5), weights)
            t = ve_(lambda e, i: e.scalar_tensor_tensor(out=c_si, in0=c_th, scalar=1.0, in1=c_t,
                                                        op0=ALU.add, op1=ALU.mult), t)
            t = ve_(lambda e, i: e.tensor_scalar(c_si, c_si, 0.5, None, ALU.mult), t)
            W2 = 2 * H
            for c in range(3):
                bank, m = fill([lambda e, i, b, k=k, c=c: e.matmul(
                    b[0:NB, :], c_si[:, k, :], wmod[:, k, c * W2:(c + 1) * W2], start=k == 0, stop=k == 1)
                    for k in range(2)], t)
                freed(ve_(lambda e, i, c=c, bank=bank: e.tensor_copy(modr[:, c * W2:(c + 1) * W2], bank[0:NB, :]), m))
            t = work["free"][work["k"]]
            rows = []
            for q in (1, 4):
                rows.append(ve_(lambda e, i, q=q: e.tensor_scalar(
                    modr[:, q * H:(q + 1) * H], modr[:, q * H:(q + 1) * H], 1.0, None, ALU.add), t))
            for q in (2, 5):
                g = modr[:, q * H:(q + 1) * H]
                prev = rows[-1]
                t1 = sc(lambda e, i, g=g: e.activation(gabs, g, ACT.Abs), t, prev)
                t1 = ve_(lambda e, i: e.tensor_scalar(gabs, gabs, 0.25, None, ALU.max), t1)
                t2 = ve_(lambda e, i, g=g: e.tensor_scalar(gsgn, g, 0.0, 2.0, ALU.is_ge, ALU.mult), prev)
                rows.append(ve_(lambda e, i, g=g: e.scalar_tensor_tensor(
                    out=g, in0=gsgn, scalar=-1.0, in1=gabs, op0=ALU.add, op1=ALU.mult), t1, t2))
            last["mod"] = pr.dma("sync", "out", lambda e, i: e.dma_start(mod_dram, modr[:, 0:NMOD * H]), rows)

            chunks = []
            for q in range(0, E, 4):
                chunks.append((d["L0_ffn_gate_proj"][q:q + 4].rearrange("e i h -> i e h"), gate_t[:, q:q + 4, :, :], False))
                chunks.append((d["L0_ffn_up_proj"][q:q + 4].rearrange("e i h -> i e h"), up_t[:, q:q + 4, :, :], False))
                chunks.append((d["L0_ffn_down_proj"][q:q + 4].rearrange("e (k h) i -> h e k i", h=P),
                               down_t[:, q:q + 4, :], True))
            free = [None] * 3
            for n, (src, dst, split) in enumerate(chunks):
                s = stage[n % 3]
                if split:
                    tgt = s.rearrange("p (e k i) -> p e k i", e=4, k=HK)
                    ld = None
                    for q in range(4):
                        ld = pr.dma("sync", f"stage{n % 3}", lambda e, i, q=q, tgt=tgt, src=src: e.dma_start(tgt[:, q], src[:, q]), [free[n % 3]])
                else:
                    tgt = s.rearrange("p (e h) -> p e h", e=4)
                    ld = pr.dma("sync", f"stage{n % 3}", lambda e, i, tgt=tgt, src=src: e.dma_start(tgt, src), [free[n % 3]])
                for half in range(2):
                    bank, m = fill([lambda e, i, b, c=c, s=s, half=half: e.transpose(
                        b[:, c * P:(c + 1) * P], s[:, (4 * half + c) * P:(4 * half + c + 1) * P], ident[:, :])
                        for c in range(4)], ld, last["ident"])
                    if split:
                        o = dst[:, 2 * half:2 * half + 2, :].rearrange("p e h -> p (e h)")
                    else:
                        o = dst[:, 2 * half:2 * half + 2, :, :].rearrange("p e k i -> p (e k i)")
                    if half:
                        f = ve_(lambda e, i, o=o, bank=bank: e.tensor_copy(o, bank[:, :]), m)
                    else:
                        f = sc(lambda e, i, o=o, bank=bank: e.activation(o, bank[:, :], ACT.Copy), m)
                    freed(f)
                free[n % 3] = m

        def norm_rows(src, dst, stats, after, free_dst):
            s_, m_, v_, r_ = stats
            toks = [ve_(lambda e, i, t=t: e.bn_stats(s_[:, t, :], src[:, t, :]), after) for t in range(TT)]
            yield
            pause(toks[-1])
            toks = [ve_(lambda e, i, t=t: e.bn_aggr(m_[:, t, :], s_[:, t, :])) for t in range(TT)]
            t1 = ve_(lambda e, i: e.tensor_scalar(v_[:, :], m_[:, :, 1], EPS, None, ALU.add), toks[-1])
            t2 = po(lambda e, i: e.tensor_tensor(r_[:, :], v_[:, :], minus_half[:, :], ALU.pow), t1, last["const"])
            yield
            for t in range(TT):
                tok = ve_(lambda e, i, t=t: e.tensor_scalar(dst[:, t, :], src[:, t, :], m_[:, t, 0:1], r_[:, t:t + 1],
                                                            ALU.subtract, ALU.mult), t2, free_dst)
            yield
            return tok

        def split3(bank, filled, stack, free_stack):
            a = sc(lambda e, i: e.activation(stack[:, :], bank[0:SPLIT * FULL, :], ACT.Copy), filled, free_stack)
            yield
            r = freed(ve_(lambda e, i: e.tensor_tensor(rest, bank[0:SPLIT * FULL, :], stack[:, :], ALU.subtract),
                          a, last.get("rest"), last.get("conv0")), bank)
            yield
            s2 = sc(lambda e, i: e.activation(second[:, :], rest, ACT.Copy), r)
            p1 = sc(lambda e, i: e.activation(stack[FULL:2 * FULL, :], second[FULL:2 * FULL, :], ACT.Copy), s2)
            r2 = ve_(lambda e, i: e.tensor_tensor(rest[2 * FULL:], rest[2 * FULL:], second[2 * FULL:, :],
                                                 ALU.subtract), s2)
            yield
            done = sc(lambda e, i: e.activation(stack[2 * FULL:, :], rest[2 * FULL:], ACT.Copy), r2, p1)
            last["rest"] = last["conv0"] = [done, r2]
            return done

        def take(row, i, a, b):
            return mod_dram[bass.ds(row(i), 1), a * H:b * H]

        def prepare(row):
            ld = pr.dma("sync", "x", lambda e, i: e.dma_start(
                xt[:, :, :], d["L0_attn_x"].rearrange("b (t p) h -> p b t h", p=P)[:, bass.ds(row(i), 1), :, :].rearrange(
                    "p b t h -> p (b t) h")), [last.get("base")])
            md = pr.dma("sync", "mods", lambda e, i: e.dma_start(
                mod_row[:, :, :].rearrange("p a h -> p (a h)"), take(row, i, 0, 2).to_broadcast([P, 2 * H])),
                [last["mod"], last.get("h")])
            yield
            normed = yield from norm_rows(xt, ht, (st, mv, ve, rstd), ld, last.get("base"))
            t = po(lambda e, i: e.tensor_tensor(ht[:, :, :], ht[:, :, :],
                                                mod_row[:, 1:2, :].to_broadcast([P, TT, H]), ALU.mult),
                   normed, md)
            yield
            t = po(lambda e, i: e.tensor_tensor(ht[:, :, :], ht[:, :, :],
                                                mod_row[:, 0:1, :].to_broadcast([P, TT, H]), ALU.add), t)
            last["h"] = t
            yield
            normed = last["normed_h"] = yield from norm_rows(ht, z2, (st, mv, ve, rstd), t, last.get("z2_read"))
            for k in range(HK):
                bank, m = fill([lambda e, i, b, t=t_, k=k: e.transpose(
                    b[:, t * P:(t + 1) * P], z2[:, t, k * P:(k + 1) * P], ident[:, :]) for t_ in range(TT)],
                    normed, last["ident"])
                last["z2_read"] = m
                last["xn"] = freed(sc(lambda e, i, k=k, bank=bank: e.activation(
                    xn_t[:, k, :], bank[:, :], ACT.Identity, bias=n_bias[:, k:k + 1], scale=n_scale[:, k:k + 1]),
                    m, last.get("xn_read")))
                yield

        def silu_inputs():
            for q in range(DK):
                cv = conv[:, q % 2, :]
                bank, m = fill([lambda e, i, b, k=k, q=q: e.matmul(
                    b[:, :], w_in[:, k, q * P:(q + 1) * P], xn_t[:, k, :], start=k == 0, stop=k == HK - 1)
                    for k in range(HK)], last["xn"])
                last["xn_read"] = m
                t0 = sc(lambda e, i, q=q, cv=cv, bank=bank: e.activation(
                    cv, bank[:, :], ACT.Identity, bias=conv_b[:, q:q + 1], scale=conv_w[:, q, 1:2]),
                    m, last.get(f"conv{q % 2}"), last["halved"])
                yield
                t0 = ve_(lambda e, i, q=q, cv=cv, bank=bank: e.scalar_tensor_tensor(
                    out=cv[:, 1:T], in0=bank[:, 0:T - 1], scalar=conv_w[:, q, 0:1], in1=cv[:, 1:T],
                    op0=ALU.mult, op1=ALU.add), t0, last["halved"])
                t0 = freed(ve_(lambda e, i, q=q, cv=cv, bank=bank: e.scalar_tensor_tensor(
                    out=cv[:, 0:T - 1], in0=bank[:, 1:T], scalar=conv_w[:, q, 2:3], in1=cv[:, 0:T - 1],
                    op0=ALU.mult, op1=ALU.add), t0), bank)
                t1 = sc(lambda e, i, q=q, cv=cv: e.activation(xb[:, q, :], cv, ACT.Tanh), t0, last.get("xb_read"))
                yield
                last[f"conv{q % 2}"] = last["xb"] = ve_(lambda e, i, q=q, cv=cv: e.scalar_tensor_tensor(
                    out=xb[:, q, :], in0=xb[:, q, :], scalar=1.0, in1=cv, op0=ALU.add, op1=ALU.mult), t1)

        def step_sizes(q):
            pair = slice(2 * q, 2 * q + 2)
            for m_ in (2 * q, 2 * q + 1):
                bank, m = fill([lambda e, i, b, k=k, m_=m_: e.matmul(
                    b[:, :], w_dt[:, k, m_ * P:(m_ + 1) * P], xb[:, k, :], start=k == 0, stop=k == DK - 1)
                    for k in range(DK)], last["xb"])
                t0 = sc(lambda e, i, m_=m_, bank=bank: e.activation(
                    dtx[:, m_, :], bank[:, :], ACT.Abs, bias=b_dt[:, m_:m_ + 1]), m, last.get(f"drive{q}"))
                t1 = freed(sc(lambda e, i, m_=m_, bank=bank: e.activation(
                    dt[:, m_, :], bank[:, :], ACT.Relu, bias=b_dt[:, m_:m_ + 1]), last.get(f"decay{q}"), last["mod"]),
                    bank)
                t2 = sc(lambda e, i, m_=m_: e.activation(dtx[:, m_, :], dtx[:, m_, :], ACT.Exp, scale=-1.0), t0)
                yield
            if q:
                last["xb_read"] = [m]
            t3 = sc(lambda e, i: e.activation(dtx[:, pair, :], dtx[:, pair, :], ACT.Ln, bias=1.0), t2)
            yield
            last[f"dt{q}"] = ve_(lambda e, i: e.tensor_tensor(
                dt[:, pair, :], dt[:, pair, :], dtx[:, pair, :], ALU.add), t1, t3)
            yield
            last[f"dtx{q}"] = po(lambda e, i: e.tensor_tensor(
                dtx[:, pair, :], dt[:, pair, :], xb[:, pair, :], ALU.mult), last[f"dt{q}"], last["xb"])
            if q:
                last["xb_read"].append(last["dtx1"])
            yield

        def rows_bc():
            bank, m = fill([lambda e, i, b, k=k: e.matmul(
                b[0:SPLIT * BC, :], w_bc[:, k, :], xb[:, k, :], start=k == 0, stop=k == DK - 1)
                for k in range(DK)], last["xb"])
            last["bc_next"] = yield from split3(bank, m, bc_next, last.get("bc"))
            yield

        def take_bc():
            last["bc"] = sc(lambda e, i: e.activation(bc_stack[:, :], bc_next[:, :], ACT.Copy),
                            last["bc_next"], last.get("bc_read"))
            yield

        def gates():
            for q in range(DK):
                bank, m = fill([lambda e, i, b, k=k, q=q: e.matmul(
                    b[:, :], w_in[:, k, (DK + q) * P:(DK + q + 1) * P], xn_t[:, k, :], start=k == 0, stop=k == HK - 1)
                    for k in range(HK)], last["xn"])
                last["xn_read"] = m
                t0 = sc(lambda e, i, q=q, bank=bank: e.activation(gz[:, q, :], bank[:, :], ACT.Tanh, scale=0.5),
                        m, last.get("y2_read"))
                yield
                last["gz"] = freed(ve_(lambda e, i, q=q, bank=bank: e.scalar_tensor_tensor(
                    out=gz[:, q, :], in0=gz[:, q, :], scalar=1.0, in1=bank[:, :], op0=ALU.add, op1=ALU.mult), t0), bank)
            yield

        def residual(row):
            ga = pr.dma("sync", "ga", lambda e, i: e.dma_start(
                ga_row[:, :], take(row, i, 2, 3).to_broadcast([P, H])), [last.get("x1"), last["mod"]])
            last["ga"] = ga
            yield
            t = po(lambda e, i: e.tensor_tensor(
                ht[:, :, :], ht[:, :, :], ga_row[:, :].rearrange("p (a h) -> p a h", a=1).to_broadcast(
                    [P, TT, H]), ALU.mult), ga, last["h"], last["normed_h"])
            yield
            last["base"] = po(lambda e, i: e.tensor_tensor(base[:, :, :], xt[:, :, :], ht[:, :, :], ALU.add),
                              t, last.get("x1"))
            yield

        u_done, b_done, c_done, ex_done, scan_done, g_done, add_done, sum_done = ({} for _ in range(8))

        def broadcast(g, part):
            rowi, dst, s, made, free = (
                (g % NS, b_bc, g % B_RING, b_done, u_done.get(g - B_RING)),
                (NS + g % NS, c_bc, g % C_RING, c_done, g_done.get(g - C_RING)))[part]
            bank, m = fill([lambda e, i, b: e.matmul(
                b[:, :], sel[:, rowi:rowi + 1].to_broadcast([SPLIT * FULL, P]), bc_stack[:, :],
                start=True, stop=True)], last["bc"], last["sel"])
            last["bc_read"] = m
            made[g] = freed(sc(lambda e, i: e.activation(dst[:, s, :], bank[:, :], ACT.Copy), m, free), bank)

        def drive(g):
            q, r, s = g % NU // NS, g % RING, g % B_RING
            u_done[g] = last[f"drive{q}"] = po(lambda e, i: e.tensor_tensor(
                unit[:, r, :, :], dtx[:, 2 * q:2 * q + 2, :], b_bc[:, s:s + 1, :].to_broadcast([P, 2, T]), ALU.mult),
                b_done[g], last[f"dtx{q}"], sum_done.get(g // 2 - RING // 2))

        def decay(g):
            q, n = g % NU // NS, g % NS
            for a in range(2):
                ex_done[g, a] = last[f"decay{q}"] = sc(lambda e, i, a=a: e.activation(
                    decays[:, a, :], dt[:, 2 * q + a, :], ACT.Exp, scale=a_neg[:, 2 * q + a, n:n + 1]),
                    last[f"dt{q}"], scan_done.get((g - 1, a)))

        def recur(g):
            r = g % RING
            for a in range(2):
                scan_done[g, a] = ve_(lambda e, i, a=a: e.tensor_tensor_scan(
                    unit[:, r, a, :], decays[:, a, :], unit[:, r, a, :], 0.0, ALU.mult, ALU.add),
                    ex_done[g, a], u_done[g])

        def times_c(g):
            r, s = g % RING, g % C_RING
            g_done[g] = ve_(lambda e, i: e.tensor_tensor(
                unit[:, r, :, :], unit[:, r, :, :], c_bc[:, s:s + 1, :].to_broadcast([P, 2, T]), ALU.mult),
                scan_done[g, 1], c_done[g])

        def add_pair(g):
            r0, r1 = (g - 1) % RING, g % RING
            if g % 2:
                add_done[g // 2] = po(lambda e, i: e.tensor_tensor(
                    unit[:, r0, :, :], unit[:, r0, :, :], unit[:, r1, :, :], ALU.add), g_done[g])

        def sum_pair(g):
            if not g % 2:
                return
            p, r0, q = g // 2, (g - 1) % RING, g % NU // NS
            first, final = g % NS == 1, g % NS == NS - 1
            for a in range(2):
                if first:
                    m_ = 2 * q + a
                    last["diag_read"] = pe(lambda e, i, a=a, m_=m_: e.matmul(
                        ybank[:, a, :], diag_d[:, m_, :], xb[:, m_, :], start=True, stop=False),
                        last["xb"], last["diag"], last.get("y_read"))
                sum_done[p] = pe(lambda e, i, a=a: e.matmul(
                    ybank[:, a, :], ident[:, :], unit[:, r0, a, :], start=False, stop=final), add_done[p])
            if first and q:
                last["xb_read"].append(last["diag_read"])

        def gate_y(g):
            q = g % NU // NS
            for a in range(2):
                last["y2"] = last["y_read"] = ve_(lambda e, i, a=a: e.tensor_tensor(
                    gz[:, 2 * q + a, :], gz[:, 2 * q + a, :], ybank[:, a, :], ALU.mult),
                    sum_done[g // 2], last["gz"])

        def beside(k, streams):
            for gen, steps, first, final in streams:
                if first <= k <= final:
                    n = final - first + 1
                    for _ in range((k - first + 1) * steps // n - (k - first) * steps // n):
                        next(gen, None)
                if k == final:
                    assert next(gen, "spent") == "spent", (first, final)

        def row_units(index, streams, experts=None, run=True):
            def half_step(k):
                if experts and k >= EXPERTS_FROM:
                    experts.half_step()

            for k in range(NU if run else 4):
                g = index * NU + k
                if run:
                    recur(g)
                    decay(g + 1)
                if k % NS == 3 and g > 3:
                    gate_y(g - 4)
                half_step(k)
                if run:
                    broadcast(g + 2, 1)
                if g >= 1 and (run or k < 1):
                    times_c(g - 1)
                if g >= 2 and (run or k < 2):
                    add_pair(g - 2)
                beside(2 * k, streams)
                half_step(k)
                if run:
                    broadcast(g + 3, 0)
                    drive(g + 3)
                if g >= 3 and (run or k < 3):
                    sum_pair(g - 3)
                beside(2 * k + 1, streams)
                half_step(k)
            if experts:
                experts.finish_steps()

        def first_units():
            for g in range(3):
                broadcast(g, 0)
                drive(g)
            broadcast(0, 1)
            broadcast(1, 1)
            decay(0)

        def project():
            for h in range(2):
                tiles = slice(h * TT // 2, (h + 1) * TT // 2)
                bank, m = fill([lambda e, i, b, t=t, k=k, h=h: e.matmul(
                    b[:, t * H:(t + 1) * H], gz[:, k, (h * TT // 2 + t) * P:(h * TT // 2 + t + 1) * P], w_out[:, k, :],
                    start=k == 0, stop=k == DK - 1) for t in range(TT // 2) for k in range(DK)],
                    last["y2"], last["halved"])
                last["y2_read"] = m
                yield
                t0 = freed(ve_(lambda e, i, bank=bank, tiles=tiles: e.tensor_tensor(
                    x1[:, tiles, :], bank[:, :].rearrange("p (t h) -> p t h", h=H), ga_row[:, :].rearrange(
                        "p (a h) -> p a h", a=1).to_broadcast([P, TT // 2, H]), ALU.mult),
                    m, last["ga"], last.get("moe_add")), bank)
                last["x1"] = ve_(lambda e, i, tiles=tiles: e.tensor_tensor(
                    x1[:, tiles, :], x1[:, tiles, :], base[:, tiles, :], ALU.add), t0, last["base"])

        def load_modulation(row):
            last["gb"] = pr.dma("sync", "gb", lambda e, i: e.dma_start(
                gb_row[:, :], take(row, i, 5, 6).to_broadcast([P, H])), [last.get("gb_read")])
            last["cols"] = pr.dma("sync", "cols", lambda e, i: e.dma_start(
                mod_col[:, :], take(row, i, 3, 5).rearrange("b (q p) -> p (b q)", p=P)), [last.get("h2")])

        def route(row):
            normed = yield from norm_rows(x1, z2, (st2, mv2, ve2, rstd2), last["x1"], last.get("z2_read"))
            for k in range(HK):
                bank, m = fill([lambda e, i, b, t=t_, k=k: e.transpose(
                    b[:, t * P:(t + 1) * P], z2[:, t, k * P:(k + 1) * P], ident[:, :]) for t_ in range(TT)], normed)
                last["z2_read"] = m
                h2 = freed(sc(lambda e, i, k=k, bank=bank: e.activation(
                    h2_t[:, k, :], bank[:, :], ACT.Identity, bias=mod_col[:, k:k + 1],
                    scale=mod_col[:, HK + k:HK + k + 1]), m, last["cols"], last.get("h2_read")))
                yield
            last["h2"] = h2
            bank, m = fill([lambda e, i, b, t=t_, k=k: e.matmul(
                b[:, t * E:(t + 1) * E], h2_t[:, k, t * P:(t + 1) * P], router_t[:, k, :],
                start=k == 0, stop=k == HK - 1) for t_ in range(TT) for k in range(HK)], h2)
            t = freed(sc(lambda e, i, bank=bank: e.activation(
                r_th[:, :, :].rearrange("p t e -> p (t e)"), bank[:, 0:TT * E], ACT.Tanh, scale=0.5), m))
            yield
            s = ve_(lambda e, i: e.tensor_scalar(r_s[:, :, :], r_th[:, :, :], 0.5, 0.5, ALU.mult, ALU.add), t)
            t = ve_(lambda e, i: e.tensor_tensor(r_ch[:, :, :], r_s[:, :, :], e_bias[:, :].rearrange(
                "p (a e) -> p a e", a=1).to_broadcast([P, TT, E]), ALU.add), s)
            yield
            pairs = r_ch[:, :, :].rearrange("p t (g m) -> p (t g) m", m=GRP)
            hi = ve_(lambda e, i: e.tensor_tensor(r_hi[:, :, :], pairs[:, :, 0:2], pairs[:, :, 2:4], ALU.max), t)
            lo = ve_(lambda e, i: e.tensor_tensor(r_lo[:, :, :], pairs[:, :, 0:2], pairs[:, :, 2:4], ALU.min), t)
            top = ve_(lambda e, i: e.tensor_tensor(r_top[:, :], r_hi[:, :, 0], r_hi[:, :, 1], ALU.max), hi)
            m2 = ve_(lambda e, i: e.tensor_tensor(r_m2[:, :], r_hi[:, :, 0], r_hi[:, :, 1], ALU.min), hi)
            m3 = ve_(lambda e, i: e.tensor_tensor(r_m3[:, :], r_lo[:, :, 0], r_lo[:, :, 1], ALU.max), lo)
            t = ve_(lambda e, i: e.tensor_tensor(r_m2[:, :], r_m2[:, :], r_m3[:, :], ALU.max), m2, m3)
            t = ve_(lambda e, i: e.tensor_tensor(r_g[:, :], r_top[:, :], r_m2[:, :], ALU.add), top, t)
            yield
            g = r_g[:, :].rearrange("p (t g) -> p t g", g=NGRP)
            this = g.rearrange("p t (g a) -> p t g a", a=1).to_broadcast([P, TT, NGRP, NGRP])
            other = g.rearrange("p t (a g) -> p t a g", a=1).to_broadcast([P, TT, NGRP, NGRP])
            low = lower[:, :, :].rearrange("p (a j) i -> p a j i", a=1).to_broadcast([P, TT, NGRP, NGRP])
            gt = ve_(lambda e, i: e.tensor_tensor(r_gt[:, :, :, :], other, this, ALU.is_gt), t)
            t = ve_(lambda e, i: e.tensor_tensor(r_eq[:, :, :, :], other, this, ALU.is_equal), t)
            t = ve_(lambda e, i: e.tensor_tensor(r_eq[:, :, :, :], r_eq[:, :, :, :], low, ALU.mult), t)
            t = ve_(lambda e, i: e.tensor_tensor(r_gt[:, :, :, :], r_gt[:, :, :, :], r_eq[:, :, :, :], ALU.add), t, gt)
            t = ve_(lambda e, i: e.tensor_reduce(r_cnt[:, :], r_gt[:, :, :, :].rearrange("p t j i -> p (t j) i"),
                                                 AX.X, ALU.add), t)
            t = ve_(lambda e, i: e.tensor_scalar(r_msk[:, :], r_cnt[:, :], 1.5, None, ALU.is_lt), t)
            t = ve_(lambda e, i: e.tensor_tensor(
                r_tmp[:, :, 0:E].rearrange("p t (g m) -> p t g m", m=GRP),
                pairs.rearrange("p (t g) m -> p t g m", t=TT),
                r_msk[:, :].rearrange("p (t g a) -> p t g a", t=TT, a=1).to_broadcast([P, TT, NGRP, GRP]),
                ALU.mult), t)
            yield
            pause(t)
            ms = [ve_(lambda e, i, q=q: e.max(r_m8[:, q, :], r_tmp[:, q, 0:E])) for q in range(TT)]
            t8 = ve_(lambda e, i: e.memset(r_m8[:, :, 4:8], NEG), ms[-1])
            pause(t8)
            for q in range(TT):
                t = ve_(lambda e, i, q=q: e.match_replace(r_cut[:, q, :], r_m8[:, q, :], r_tmp[:, q, :], 1.0e38))
            t = ve_(lambda e, i: e.tensor_tensor(r_sel[:, :, :], r_cut[:, :, 0:E], r_tmp[:, :, 0:E], ALU.not_equal), t)
            w = ve_(lambda e, i: e.tensor_tensor(r_w[:, :, :], r_s[:, :, :], r_sel[:, :, :], ALU.mult), t)
            t = ve_(lambda e, i: e.tensor_reduce(r_den[:, :], r_w[:, :, :], AX.X, ALU.add), w)
            t = ve_(lambda e, i: e.tensor_scalar(r_den[:, :], r_den[:, :], 1e-20, 2.0, ALU.add, ALU.mult), t)
            t = ve_(lambda e, i: e.reciprocal(r_rec[:, :], r_den[:, :]), t)
            for s_ in range(SPLIT):
                t3 = ve_(lambda e, i, s_=s_: e.tensor_tensor(
                    w3[:, :, s_ * FULL:s_ * FULL + E], r_w[:, :, :],
                    r_rec[:, :].rearrange("p (t a) -> p t a", a=1).to_broadcast([P, TT, E]), ALU.mult),
                    t, last.get("w3_read"), last["const"])
            yield
            bank, m = fill([lambda e, i, b, t=t_: e.transpose(
                b[0:SPLIT * FULL, t * P:(t + 1) * P], w3[:, t, :], ident[:, :]) for t_ in range(TT)], t3)
            last["w3_read"] = m
            last["w"] = yield from split3(bank, m, w_stack, last.get("w_read"))
            yield

        class Experts:

            def __init__(self, row):
                self.row = row
                self.up, self.act, self.w, self.downs, self.bank = {}, {}, {}, {}, {}
                self.done = 0

            def half_step(self):
                s = self.done // 2
                if self.done % 2 == 0:
                    self.gate(s - 1)
                    self.scale(s - 2)
                    self.products(s)
                else:
                    self.combine(s - 1)
                    self.down(s - 2)
                    self.weigh(s - 1)
                self.done += 1

            def finish_steps(self):
                while self.done < 2 * (2 * E + 2):
                    self.half_step()

            def ok(self, s):
                return 0 <= s < 2 * E

            def weigh(self, s):
                if not self.ok(s):
                    return
                e_, h = s % E, s // E
                bank, m = fill([lambda e, i, b: e.matmul(
                    b[:, 0:HT], sel[:, e_:e_ + 1].to_broadcast([SPLIT * FULL, P]), w_stack[:, h * HT:(h + 1) * HT], start=True, stop=True)], last["w"])
                last["w_read"] = m
                self.w[s] = freed(sc(lambda e, i: e.activation(w_all[:, s % 2, :], bank[:, 0:HT], ACT.Copy), m,
                                     self.act.get(s - 2) or last.get("act")))

            def products(self, s):
                if not self.ok(s):
                    return
                e_, x = s % E, slice(s // E * HT, (s // E + 1) * HT)
                bank, m = fill([lambda e, i, b, k=k, c=c, w=w: e.matmul(
                    b[:, c * HT:(c + 1) * HT], w[:, e_, k, :], h2_t[:, k, x], start=k == 0, stop=k == HK - 1)
                    for c, w in enumerate((gate_t, up_t)) for k in range(HK)], last["h2"], ring="experts")
                last["h2_read"] = m
                self.bank[s] = (bank, m)

            def gate(self, s):
                if not self.ok(s):
                    return
                bank, m = self.bank[s]
                self.bank[s] += (sc(lambda e, i: e.activation(etanh[:, s % 2, :], bank[:, 0:HT], ACT.Tanh, scale=0.5),
                                    m, last.get(f"etanh{s % 2}")),)

            def combine(self, s):
                if not self.ok(s):
                    return
                bank, m, t0 = self.bank[s]
                a = act[:, s % MOE_RING, :]
                t1 = ve_(lambda e, i: e.scalar_tensor_tensor(
                    out=a, in0=etanh[:, s % 2, :], scalar=1.0, in1=bank[:, 0:HT], op0=ALU.add, op1=ALU.mult),
                    t0, self.downs.get(s - MOE_RING) or last.get("down"))
                last[f"etanh{s % 2}"] = t1
                self.up[s] = freed(ve_(lambda e, i: e.tensor_tensor(a, a, bank[:, HT:2 * HT], ALU.mult), t1), bank)

            def scale(self, s):
                if not self.ok(s):
                    return
                a = act[:, s % MOE_RING, :]
                self.act[s] = ve_(lambda e, i: e.tensor_tensor(a, a, w_all[:, s % 2, :], ALU.mult),
                                  self.up[s], self.w[s])
                last["act"] = self.act[s]

            def down(self, s):
                if not self.ok(s):
                    return
                e_, h = s % E, s // E
                for t in range(TT // 2):
                    last["down"] = self.downs[s] = pe(lambda e, i, t=t: e.matmul(
                        mbank[:, t * H:(t + 1) * H], act[:, s % MOE_RING, t * P:(t + 1) * P], down_t[:, e_, :],
                        start=(e_ == 0 and t == 0), stop=(e_ == E - 1), skip_group_check=True),
                        self.act[s], last.get("moe_read"))
                if e_ == E - 1:
                    self.finish(h)

            def finish(self, h):
                tiles = slice(h * TT // 2, (h + 1) * TT // 2)
                mo = mbank[:, :].rearrange("p (t h) -> p t h", h=H)
                t0 = ve_(lambda e, i: e.tensor_tensor(z2[:, tiles, :], mo, gb_row[:, :].rearrange(
                    "p (a h) -> p a h", a=1).to_broadcast([P, TT // 2, H]), ALU.mult), last["down"], last["gb"],
                    last["z2_read"], last.get("out"))
                last["moe_read"] = last["gb_read"] = t0
                t0 = po(lambda e, i: e.tensor_tensor(z2[:, tiles, :], z2[:, tiles, :], x1[:, tiles, :], ALU.add), t0)
                last["moe_add"] = t0
                if h == 1:
                    last["out"] = last["z2_read"] = pr.dma("sync", "out", lambda e, i: e.dma_start(
                        out.rearrange("b (t p) h -> p b t h", p=P)[:, bass.ds(self.row(i), 1), :, :].rearrange(
                            "p b t h -> p (b t) h"), z2[:, :, :]), [t0])

        def chain(*streams):
            for s in streams:
                yield from s

        pr.begin()
        setup()
        for _ in chain(prepare(lambda i: 0), silu_inputs(), rows_bc(), take_bc(), step_sizes(0)):
            pass
        first_units()

        def around(row, coming, behind=None):
            streams = [(residual(row), 4, 11, 16), (chain(gates(), step_sizes(1)), 10, 11, 25),
                       (prepare(coming), 13, 17, 37),
                       (chain(silu_inputs(), rows_bc(), step_sizes(0)), 17, 40, 57), (take_bc(), 2, 58, 58)]
            if behind is not None:
                load_modulation(behind)
                streams.insert(0, (chain(project(), route(behind)), 17, 7, 19))
            return streams

        row_units(0, around(lambda i: 0, lambda i: 1))
        pr.begin(loop=(1, NB))
        work["free"] = [pr.before("scalar", "vector")] * 5
        rings.update(work=[0, 1, 2], experts=[3, 4])
        for name in ("ident", "sel", "const", "mod", "halved", "diag"):
            last[name] = None
        for name, who in (("h2_read", "tensor"), ("w_read", "tensor"), ("down", "tensor"), ("w3_read", "tensor"),
                          ("moe_read", "vector"), ("gb_read", "vector"), ("etanh0", "vector"), ("etanh1", "vector"),
                          ("act", "vector"), ("x1", "vector"), ("y2_read", "tensor"),
                          ("h2", "scalar"), ("moe_add", "gpsimd"), ("out", "out")):
            last[name] = pr.before(who)
        last["z2_read"] = pr.before("tensor", "out")
        row_units(1, around(lambda i: i, lambda i: (i + 1) % NB, lambda i: i - 1), Experts(lambda i: i - 1))
        pr.begin()
        row_units(2, [], run=False)
        load_modulation(lambda i: NB - 1)
        for _ in chain(project(), route(lambda i: NB - 1)):
            pass
        last_row = Experts(lambda i: NB - 1)
        last_row.finish_steps()
        pr.close()

        ctx.enter_context(nc.allow_non_contiguous_dma(reason="small vectors onto partitions"))
        block = ctx.enter_context(nc.Block())

        @block.tensor
        def _(eng):
            pr.replay(eng, "tensor")

        @block.vector
        def _(eng):
            pr.replay(eng, "vector")

        @block.scalar
        def _(eng):
            pr.replay(eng, "scalar")

        @block.gpsimd
        def _(eng):
            pr.replay(eng, "gpsimd")

        @block.sync
        def _(eng):
            pr.replay(eng, "sync")
            eng.wait_ge(dma_sems["out"], pr.totals[dma_sems["out"]])


_INS = ['L0_attn_x', 'L0_attn_norm_scale', 'L0_attn_norm_bias', 'L0_attn_W_in', 'L0_attn_conv_w', 'L0_attn_conv_b',
        'L0_attn_W_dt', 'L0_attn_b_dt', 'L0_attn_A_log', 'L0_attn_D_param', 'L0_attn_W_B', 'L0_attn_W_C',
        'L0_attn_W_out', 'L0_ffn_gate_weight', 'L0_ffn_e_bias', 'L0_ffn_gate_proj', 'L0_ffn_up_proj',
        'L0_ffn_down_proj', 'L0_c', 'L0_wmod']


def kernel(**inputs):
    import numpy as _np
    import concourse.bacc as _bacc
    from concourse import mybir as _mybir
    from concourse.bass_utils import run_bass_kernel_spmd as _run

    nc = _bacc.Bacc("TRN2", target_bir_lowering=False, num_devices=1)
    arrays, aps = {}, {}
    for name in _INS:
        a = _np.ascontiguousarray(inputs[name])
        arrays[f"in_{name}_dram"] = a
        aps[name] = nc.dram_tensor(f"in_{name}_dram", a.shape, _mybir.dt.from_np(a.dtype), kind="ExternalInput").ap()
    shape = inputs["L0_attn_x"].shape
    out = nc.dram_tensor("out_0_dram", shape, _mybir.dt.float32, kind="ExternalOutput").ap()
    build(nc, aps, out)
    r = _run(nc, [arrays], core_ids=[0])
    return r.results[0]["out_0_dram"]
```

```python
from contextlib import ExitStack

import concourse.bass as bass
from concourse import mybir

F32 = mybir.dt.float32
BF16 = mybir.dt.bfloat16
ALU = mybir.AluOpType
ACT = mybir.ActivationFunctionType
AX = mybir.AxisListType

P = 128
ENGINES = ("tensor", "vector", "scalar", "gpsimd", "sync")


class Token:

    def __init__(self, engine, part, sem, step):
        self.engine, self.part, self.sem, self.step = engine, part, sem, step
        self.waited = False
        self.count = 0


class Program:

    def __init__(self, nc, sems, dma_sems):
        self.nc, self.sems, self.dma_sems = nc, sems, dma_sems
        self.parts = []

    def begin(self, loop=None):
        self.parts.append({"loop": loop, "queue": {e: [] for e in ENGINES}, "tokens": []})

    def op(self, engine, emit, after=()):
        part = self.parts[-1]
        tok = Token(engine, len(self.parts) - 1, self.sems[engine], 1)
        self._queue(part, engine, emit, after, tok)
        return tok

    def dma(self, engine, stream, emit, after=()):
        part = self.parts[-1]
        tok = Token(engine, len(self.parts) - 1, self.dma_sems[stream], 16)
        tok.waited = True
        self._queue(part, engine, emit, after, tok)
        return tok

    def _queue(self, part, engine, emit, after, tok):
        after = flat(after)
        part["queue"][engine].append((emit, after, tok))
        part["tokens"].append(tok)
        for t in after:
            t.waited = True

    def close(self):
        loop = next(n for n, part in enumerate(self.parts) if part["loop"])
        peeled, turn = self.parts[loop - 1]["tokens"], self.parts[loop]["tokens"]
        assert len(peeled) == len(turn) and all(a.sem is b.sem for a, b in zip(peeled, turn))
        for part in self.parts:
            for t in {t.sem: t for t in part["tokens"]}.values():
                t.waited = True
        for a, b in zip(peeled, turn):
            a.waited = b.waited = a.waited or b.waited
        totals = {}
        for part in self.parts:
            before = dict(totals)
            for t in part["tokens"]:
                if t.waited:
                    totals[t.sem] = totals.get(t.sem, 0) + t.step
                    t.count = totals[t.sem]
            part["per_turn"] = {s: n - before.get(s, 0) for s, n in totals.items()}
            if part["loop"]:
                part["more"] = {s: n * (part["loop"][1] - part["loop"][0] - 1) for s, n in part["per_turn"].items()}
                for s, n in part["more"].items():
                    totals[s] += n
        self.totals = totals

    def replay(self, eng, engine):
        for index, part in enumerate(self.parts):
            if part["loop"] is None:
                self._run(eng, engine, index, part, None)
            elif part["queue"][engine]:
                with eng.Fori(*part["loop"]) as i:
                    self._run(eng, engine, index, part, i)

    def _run(self, eng, engine, index, part, i):
        seen = {}
        for emit, after, tok in part["queue"][engine]:
            need = {}
            for t in after:
                value, grows = t.count, part["loop"] is not None and t.part >= index - 1
                if part["loop"] is None and t.part < index and self.parts[t.part]["loop"]:
                    value += self.parts[t.part]["more"].get(t.sem, 0)
                need[t.sem] = max(need.get(t.sem, (0, False)), (value, grows))
            for sem, (value, grows) in need.items():
                if seen.get(sem, 0) >= value:
                    continue
                seen[sem] = value
                if grows:
                    per, first = part["per_turn"][sem], part["loop"][0]
                    assert value > 0
                    eng.wait_ge(sem, i * per + (value - first * per))
                else:
                    eng.wait_ge(sem, value)
            made = emit(eng, i)
            if tok.waited:
                made.then_inc(tok.sem, tok.step)


def flat(tokens):
    if isinstance(tokens, Token):
        return [tokens]
    return [t for x in tokens or () for t in flat(x)]


def build(nc, d, out):
    NB, T, H = d["L0_attn_x"].shape
    INNER = d["L0_attn_W_dt"].shape[0]
    NS = d["L0_attn_A_log"].shape[1]
    E, I, _ = d["L0_ffn_gate_proj"].shape
    NMOD = 6
    TT, HK, DK = T // P, H // P, INNER // P
    BC = 2 * NS
    SPLIT = 3
    NGRP, GRP = 4, E // 4
    EPS = 1e-5
    NEG = -3.0e38
    NU = 2 * NS
    RING = 8
    BC_RING = 4
    MOE_RING = 3
    EXPERTS_AT = (27, 109)
    HT = T // 2
    FULL = P // 4
    assert BC == FULL and I == P and E <= FULL and DK == 4 and TT * H == 2 * T

    ctx = ExitStack()
    with ctx:
        def sb(name, shape, dt=F32):
            return ctx.enter_context(nc.sbuf_tensor(name, shape, dt))

        w_in = sb("w_in", [P, HK, 2 * INNER])
        w_dt = sb("w_dt", [P, DK, INNER])
        w_bc = sb("w_bc", [P, DK, SPLIT * BC])
        w_out = sb("w_out", [P, DK, H])
        gate_t = sb("gate_t", [P, E, HK, I])
        up_t = sb("up_t", [P, E, HK, I])
        down_t = sb("down_t", [I, E, H])
        router_t = sb("router_t", [P, HK, E])
        ident = sb("ident", [P, P])
        sel = sb("sel", [SPLIT * FULL, BC], BF16)
        conv_w = sb("conv_w", [P, DK, 3])
        conv_b = sb("conv_b", [P, DK])
        b_dt = sb("b_dt", [P, DK])
        d_par = sb("d_par", [P, DK])
        a_neg = sb("a_neg", [P, DK, NS])
        n_scale = sb("n_scale", [P, HK])
        n_bias = sb("n_bias", [P, HK])
        e_bias = sb("e_bias", [P, E])
        lower = sb("lower", [P, NGRP, NGRP])
        minus_half = sb("minus_half", [P, TT])
        xt = sb("xt", [P, TT, H])
        ht = sb("ht", [P, TT, H])
        x1 = sb("x1", [P, TT, H])
        h2_t = sb("h2_t", [P, HK, T])
        base = sb("base", [P, TT, H])
        xn_t = sb("xn_t", [P, HK, T])
        ga_row = sb("ga_row", [P, H])
        gb_row = sb("gb_row", [P, H])
        mod_col = sb("mod_col", [P, 2 * HK])
        xb = sb("xb", [P, DK, T])
        gz = sb("gz", [P, DK, T])
        dt = sb("dt", [P, DK, T])
        dtx = sb("dtx", [P, DK, T])
        unit = sb("unit", [P, RING, 2, T])
        decays = sb("decays", [P, 2, T])
        b_bc = sb("b_bc", [P, BC_RING, T])
        c_bc = sb("c_bc", [P, BC_RING, T])
        conv = sb("conv", [P, 2, T])
        z2 = sb("z2", [P, TT, H])
        diag_d = sb("diag_d", [P, DK, P])
        bc_stack = sb("bc_stack", [SPLIT * FULL, T], BF16)
        bc_next = sb("bc_next", [SPLIT * FULL, T], BF16)
        w_stack = sb("w_stack", [SPLIT * FULL, T], BF16)
        rest = conv[0:SPLIT * FULL, 0, :]
        mod_row = conv[:, 1, :].rearrange("p (a h) -> p a h", h=H)
        second = sb("second", [SPLIT * FULL, T], BF16)
        act = sb("act", [P, MOE_RING, HT])
        etanh = sb("etanh", [P, 2, HT])
        w_all = sb("w_all", [P, 2, HT])
        st = sb("st", [P, TT, 6])
        mv = sb("mv", [P, TT, 2])
        ve = sb("ve", [P, TT])
        rstd = sb("rstd", [P, TT])
        st2 = sb("st2", [P, TT, 6])
        mv2 = sb("mv2", [P, TT, 2])
        ve2 = sb("ve2", [P, TT])
        rstd2 = sb("rstd2", [P, TT])
        mark = sb("mark", [P, 1])
        r_th = sb("r_th", [P, TT, E])
        r_s = sb("r_s", [P, TT, E])
        r_ch = sb("r_ch", [P, TT, E])
        r_hi = sb("r_hi", [P, TT * NGRP, 2])
        r_lo = sb("r_lo", [P, TT * NGRP, 2])
        r_top = sb("r_top", [P, TT * NGRP])
        r_m2 = sb("r_m2", [P, TT * NGRP])
        r_m3 = sb("r_m3", [P, TT * NGRP])
        r_g = sb("r_g", [P, TT * NGRP])
        r_gt = sb("r_gt", [P, TT, NGRP, NGRP])
        r_eq = sb("r_eq", [P, TT, NGRP, NGRP])
        r_cnt = sb("r_cnt", [P, TT * NGRP])
        r_msk = sb("r_msk", [P, TT * NGRP])
        r_tmp = sb("r_tmp", [P, TT, E + 4])
        r_m8 = sb("r_m8", [P, TT, 8])
        r_cut = sb("r_cut", [P, TT, E + 4])
        r_sel = sb("r_sel", [P, TT, E])
        r_w = sb("r_w", [P, TT, E])
        r_den = sb("r_den", [P, TT])
        r_rec = sb("r_rec", [P, TT])
        w3 = sb("w3", [P, TT, SPLIT * FULL])

        ring = unit[:, :, :, :].rearrange("p r a t -> p (r a t)")
        wmod = ring[:, 0:2 * NMOD * H].rearrange("p (k n) -> p k n", k=2)
        stage = [ring[:, q * 4 * H:(q + 1) * 4 * H] for q in range(3, 6)]
        c_t = dtx[:, 0, 0:2 * NB].rearrange("p (k b) -> p k b", k=2)
        c_th = dtx[:, 0, 64:64 + 2 * NB].rearrange("p (k b) -> p k b", k=2)
        c_si = dtx[:, 0, 128:128 + 2 * NB].rearrange("p (k b) -> p k b", k=2)
        modr = dt[0:NB, :, :].rearrange("p a t -> p (a t)")
        gabs = gz[0:NB, 0, 0:H]
        gsgn = gz[0:NB, 1, 0:H]

        ybank = ctx.enter_context(nc.psum_tensor("ybank", [P, 2, T], F32))
        mbank = ctx.enter_context(nc.psum_tensor("mbank", [P, T], F32))
        wbank = [ctx.enter_context(nc.psum_tensor(f"wbank{k}", [P, T], F32)) for k in range(5)]

        mod_dram = nc.dram_tensor("mod_scratch", (NB, NMOD * H), F32, kind="Internal").ap()

        sems = {e: ctx.enter_context(nc.semaphore(f"done_{e}")) for e in ENGINES}
        dma_sems = {s: ctx.enter_context(nc.semaphore(f"dma_{s}")) for s in
                    ("weights", "stage0", "stage1", "stage2", "x", "mods", "ga", "gb", "cols", "out")}
        pr = Program(nc, sems, dma_sems)

        def pe(emit, *after):
            return pr.op("tensor", emit, after)

        def ve_(emit, *after):
            return pr.op("vector", emit, after)

        def pause(*after):
            ve_(lambda e, i: e.memset(mark[:, :], 0.0), *after)

        def sc(emit, *after):
            return pr.op("scalar", emit, after)

        def po(emit, *after):
            return pr.op("gpsimd", emit, after)

        last = {}

        rings = {"work": [0, 1, 2], "experts": [3, 4]}
        work = {"free": [None] * 5, "k": 0}

        def fill(matmuls, *after, ring="work"):
            k = next(b for b in rings[ring] if work["free"][b] != "held")
            rings[ring] = [b for b in rings[ring] if b != k] + [k]
            work["k"] = k
            tok = None
            for n, m in enumerate(matmuls):
                waits = (*after, work["free"][k]) if n == 0 else ()
                tok = pe(lambda e, i, m=m, b=wbank[k]: m(e, i, b), *waits)
            work["free"][k] = "held"
            return wbank[k], tok

        def fill_more(bank, matmuls):
            for m in matmuls:
                tok = pe(lambda e, i, m=m: m(e, i, bank))
            return tok

        def freed(tok, bank=None):
            k = work["k"] if bank is None else next(n for n, b in enumerate(wbank) if b is bank)
            work["free"][k] = tok
            return tok

        def setup():
            loads = []

            def load(dst, src):
                loads.append(pr.dma("sync", "weights", lambda e, i: e.dma_start(dst, src)))

            for k in range(2):
                load(c_t[:, k, :], d["L0_c"][:, k * P:(k + 1) * P].rearrange("b p -> p b"))
            load(wmod, d["L0_wmod"].rearrange("(k p) n -> p k n", p=P))
            load(w_in[:, :, :], d["L0_attn_W_in"].rearrange("(k p) n -> p k n", p=P))
            load(w_dt[:, :, :], d["L0_attn_W_dt"].rearrange("(k p) n -> p k n", p=P))
            for s in range(SPLIT):
                load(w_bc[:, :, s * BC:s * BC + NS], d["L0_attn_W_B"].rearrange("(k p) n -> p k n", p=P))
                load(w_bc[:, :, s * BC + NS:(s + 1) * BC], d["L0_attn_W_C"].rearrange("(k p) n -> p k n", p=P))
            load(w_out[:, :, :], d["L0_attn_W_out"].rearrange("(k p) n -> p k n", p=P))
            for k in range(HK):
                load(router_t[:, k, :], d["L0_ffn_gate_weight"][:, k * P:(k + 1) * P].rearrange("e p -> p e"))
            load(conv_w[:, :, :], d["L0_attn_conv_w"].rearrange("(k p) n -> p k n", p=P))
            load(a_neg[:, :, :], d["L0_attn_A_log"].rearrange("(k p) n -> p k n", p=P))
            for dst, src in ((conv_b, "conv_b"), (b_dt, "b_dt"), (d_par, "D_param"),
                             (n_scale, "norm_scale"), (n_bias, "norm_bias")):
                load(dst[:, :], d["L0_attn_" + src].rearrange("(k p) -> p k", p=P))
            load(e_bias[:, :], d["L0_ffn_e_bias"].rearrange("(a e) -> a e", a=1).to_broadcast([P, E]))
            weights = loads[-1]

            t = po(lambda e, i: e.memset(ident[:, :], 0.0))
            last["ident"] = po(lambda e, i: e.affine_select(
                out=ident[:, :], in_=ident[:, :], compare_op=ALU.not_equal, fill=1.0, base=0,
                pattern=[[-1, P]], channel_multiplier=1), t)
            t = po(lambda e, i: e.memset(sel[:, :], 0.0))
            for s in range(SPLIT):
                t = po(lambda e, i, s=s: e.affine_select(
                    out=sel[:, :], in_=sel[:, :], compare_op=ALU.not_equal, fill=1.0, base=-s * FULL,
                    pattern=[[-1, BC]], channel_multiplier=1), t)
            last["sel"] = t
            t = po(lambda e, i: e.memset(lower[:, :, :], 1.0))
            t = po(lambda e, i: e.affine_select(
                out=lower[:, :, :], in_=lower[:, :, :], compare_op=ALU.is_gt, fill=0.0, base=0,
                pattern=[[1, NGRP], [-1, NGRP]], channel_multiplier=0), t)
            t = po(lambda e, i: e.memset(minus_half[:, :], -0.5))
            po(lambda e, i: e.memset(w3[:, :, :], 0.0))
            last["const"] = po(lambda e, i: e.memset(r_tmp[:, :, E:], NEG))

            ve_(lambda e, i: e.tensor_scalar(conv_w[:, :, :], conv_w[:, :, :], 0.5, None, ALU.mult), weights)
            ve_(lambda e, i: e.tensor_scalar(conv_b[:, :], conv_b[:, :], 0.5, None, ALU.mult))
            ve_(lambda e, i: e.tensor_scalar(w_out[:, :, :], w_out[:, :, :], 0.5, None, ALU.mult))
            for m_ in range(DK):
                last["diag"] = ve_(lambda e, i, m_=m_: e.tensor_scalar(
                    diag_d[:, m_, :], ident[:, :], d_par[:, m_:m_ + 1], None, ALU.mult), last["ident"])
            t = sc(lambda e, i: e.activation(a_neg[:, :, :], a_neg[:, :, :], ACT.Exp), weights)
            last["halved"] = ve_(lambda e, i: e.tensor_scalar(a_neg[:, :, :], a_neg[:, :, :], -1.0, None, ALU.mult), t)

            t = sc(lambda e, i: e.activation(c_th, c_t, ACT.Tanh, scale=0.5), weights)
            t = ve_(lambda e, i: e.scalar_tensor_tensor(out=c_si, in0=c_th, scalar=1.0, in1=c_t,
                                                        op0=ALU.add, op1=ALU.mult), t)
            t = ve_(lambda e, i: e.tensor_scalar(c_si, c_si, 0.5, None, ALU.mult), t)
            W2 = 2 * H
            for c in range(3):
                bank, m = fill([lambda e, i, b, k=k, c=c: e.matmul(
                    b[0:NB, :], c_si[:, k, :], wmod[:, k, c * W2:(c + 1) * W2], start=k == 0, stop=k == 1)
                    for k in range(2)], t)
                freed(ve_(lambda e, i, c=c, bank=bank: e.tensor_copy(modr[:, c * W2:(c + 1) * W2], bank[0:NB, :]), m))
            t = work["free"][work["k"]]
            rows = []
            for q in (1, 4):
                rows.append(ve_(lambda e, i, q=q: e.tensor_scalar(
                    modr[:, q * H:(q + 1) * H], modr[:, q * H:(q + 1) * H], 1.0, None, ALU.add), t))
            for q in (2, 5):
                g = modr[:, q * H:(q + 1) * H]
                prev = rows[-1]
                t1 = sc(lambda e, i, g=g: e.activation(gabs, g, ACT.Abs), t, prev)
                t1 = ve_(lambda e, i: e.tensor_scalar(gabs, gabs, 0.25, None, ALU.max), t1)
                t2 = ve_(lambda e, i, g=g: e.tensor_scalar(gsgn, g, 0.0, 2.0, ALU.is_ge, ALU.mult), prev)
                rows.append(ve_(lambda e, i, g=g: e.scalar_tensor_tensor(
                    out=g, in0=gsgn, scalar=-1.0, in1=gabs, op0=ALU.add, op1=ALU.mult), t1, t2))
            last["mod"] = pr.dma("sync", "out", lambda e, i: e.dma_start(mod_dram, modr[:, 0:NMOD * H]), rows)

            chunks = []
            for q in range(0, E, 4):
                chunks.append((d["L0_ffn_gate_proj"][q:q + 4].rearrange("e i h -> i e h"), gate_t[:, q:q + 4, :, :], False))
                chunks.append((d["L0_ffn_up_proj"][q:q + 4].rearrange("e i h -> i e h"), up_t[:, q:q + 4, :, :], False))
                chunks.append((d["L0_ffn_down_proj"][q:q + 4].rearrange("e (k h) i -> h e k i", h=P),
                               down_t[:, q:q + 4, :], True))
            free = [None] * 3
            for n, (src, dst, split) in enumerate(chunks):
                s = stage[n % 3]
                if split:
                    tgt = s.rearrange("p (e k i) -> p e k i", e=4, k=HK)
                    ld = None
                    for q in range(4):
                        ld = pr.dma("sync", f"stage{n % 3}", lambda e, i, q=q, tgt=tgt, src=src: e.dma_start(
                            tgt[:, q], src[:, q]), [free[n % 3]])
                else:
                    tgt = s.rearrange("p (e h) -> p e h", e=4)
                    ld = pr.dma("sync", f"stage{n % 3}", lambda e, i, tgt=tgt, src=src: e.dma_start(tgt, src), [free[n % 3]])
                for half in range(2):
                    bank, m = fill([lambda e, i, b, c=c, s=s, half=half: e.transpose(
                        b[:, c * P:(c + 1) * P], s[:, (4 * half + c) * P:(4 * half + c + 1) * P], ident[:, :])
                        for c in range(4)], ld, last["ident"])
                    if split:
                        o = dst[:, 2 * half:2 * half + 2, :].rearrange("p e h -> p (e h)")
                    else:
                        o = dst[:, 2 * half:2 * half + 2, :, :].rearrange("p e k i -> p (e k i)")
                    if half:
                        f = ve_(lambda e, i, o=o, bank=bank: e.tensor_copy(o, bank[:, :]), m)
                    else:
                        f = sc(lambda e, i, o=o, bank=bank: e.activation(o, bank[:, :], ACT.Copy), m)
                    freed(f)
                free[n % 3] = m

        def norm_rows(src, dst, stats, after, free_dst):
            s_, m_, v_, r_ = stats
            toks = [ve_(lambda e, i, t=t: e.bn_stats(s_[:, t, :], src[:, t, :]), after) for t in range(TT)]
            yield
            pause(toks[-1])
            toks = [ve_(lambda e, i, t=t: e.bn_aggr(m_[:, t, :], s_[:, t, :])) for t in range(TT)]
            t1 = ve_(lambda e, i: e.tensor_scalar(v_[:, :], m_[:, :, 1], EPS, None, ALU.add), toks[-1])
            t2 = po(lambda e, i: e.tensor_tensor(r_[:, :], v_[:, :], minus_half[:, :], ALU.pow), t1, last["const"])
            yield
            for t in range(TT):
                tok = ve_(lambda e, i, t=t: e.tensor_scalar(dst[:, t, :], src[:, t, :], m_[:, t, 0:1], r_[:, t:t + 1],
                                                            ALU.subtract, ALU.mult), t2, free_dst)
            yield
            return tok

        def split3(bank, filled, stack, free_stack):
            a = sc(lambda e, i: e.activation(stack[:, :], bank[0:SPLIT * FULL, :], ACT.Copy), filled, free_stack)
            yield
            r = freed(ve_(lambda e, i: e.tensor_tensor(rest, bank[0:SPLIT * FULL, :], stack[:, :], ALU.subtract),
                          a, last.get("rest"), last.get("conv0")), bank)
            yield
            s2 = sc(lambda e, i: e.activation(second[:, :], rest, ACT.Copy), r)
            p1 = sc(lambda e, i: e.activation(stack[FULL:2 * FULL, :], second[FULL:2 * FULL, :], ACT.Copy), s2)
            r2 = ve_(lambda e, i: e.tensor_tensor(rest[2 * FULL:], rest[2 * FULL:], second[2 * FULL:, :],
                                                 ALU.subtract), s2)
            yield
            done = sc(lambda e, i: e.activation(stack[2 * FULL:, :], rest[2 * FULL:], ACT.Copy), r2, p1)
            last["rest"] = last["conv0"] = [done, r2]
            return done

        def take(row, i, a, b):
            return mod_dram[bass.ds(row(i), 1), a * H:b * H]

        def prepare(row):
            ld = pr.dma("sync", "x", lambda e, i: e.dma_start(
                xt[:, :, :], d["L0_attn_x"].rearrange("b (t p) h -> p b t h", p=P)[:, bass.ds(row(i), 1), :, :].rearrange(
                    "p b t h -> p (b t) h")), [last.get("base")])
            md = pr.dma("sync", "mods", lambda e, i: e.dma_start(
                conv[:, 1, :], take(row, i, 0, 2).to_broadcast([P, 2 * H])),
                [last["mod"], last.get("conv1")])
            yield
            normed = yield from norm_rows(xt, ht, (st, mv, ve, rstd), ld, last.get("base"))
            t = po(lambda e, i: e.tensor_tensor(ht[:, :, :], ht[:, :, :],
                                                mod_row[:, 1:2, :].to_broadcast([P, TT, H]), ALU.mult),
                   normed, md)
            yield
            t = po(lambda e, i: e.tensor_tensor(ht[:, :, :], ht[:, :, :],
                                                mod_row[:, 0:1, :].to_broadcast([P, TT, H]), ALU.add), t)
            last["h"] = last["conv1"] = t
            yield
            normed = last["normed_h"] = yield from norm_rows(ht, z2, (st, mv, ve, rstd), t, last.get("z2_read"))
            for k in range(HK):
                bank, m = fill([lambda e, i, b, t=t_, k=k: e.transpose(
                    b[:, t * P:(t + 1) * P], z2[:, t, k * P:(k + 1) * P], ident[:, :]) for t_ in range(TT)],
                    normed, last["ident"])
                last["z2_read"] = m
                last["xn"] = freed(sc(lambda e, i, k=k, bank=bank: e.activation(
                    xn_t[:, k, :], bank[:, :], ACT.Identity, bias=n_bias[:, k:k + 1], scale=n_scale[:, k:k + 1]),
                    m, last.get("xn_read")))
                yield

        def silu_inputs():
            for q in range(DK):
                cv = conv[:, q % 2, :]
                bank, m = fill([lambda e, i, b, k=k, q=q: e.matmul(
                    b[:, :], w_in[:, k, q * P:(q + 1) * P], xn_t[:, k, :], start=k == 0, stop=k == HK - 1)
                    for k in range(HK)], last["xn"])
                last["xn_read"] = m
                yield
                t0 = sc(lambda e, i, q=q, cv=cv, bank=bank: e.activation(
                    cv, bank[:, :], ACT.Identity, bias=conv_b[:, q:q + 1], scale=conv_w[:, q, 1:2]),
                    m, last.get(f"conv{q % 2}"), last["halved"])
                yield
                t0 = ve_(lambda e, i, q=q, cv=cv, bank=bank: e.scalar_tensor_tensor(
                    out=cv[:, 1:T], in0=bank[:, 0:T - 1], scalar=conv_w[:, q, 0:1], in1=cv[:, 1:T],
                    op0=ALU.mult, op1=ALU.add), t0, last["halved"])
                t0 = freed(ve_(lambda e, i, q=q, cv=cv, bank=bank: e.scalar_tensor_tensor(
                    out=cv[:, 0:T - 1], in0=bank[:, 1:T], scalar=conv_w[:, q, 2:3], in1=cv[:, 0:T - 1],
                    op0=ALU.mult, op1=ALU.add), t0), bank)
                t1 = sc(lambda e, i, q=q, cv=cv: e.activation(xb[:, q, :], cv, ACT.Tanh), t0, last.get("xb_read"))
                yield
                last[f"conv{q % 2}"] = last["xb"] = ve_(lambda e, i, q=q, cv=cv: e.scalar_tensor_tensor(
                    out=xb[:, q, :], in0=xb[:, q, :], scalar=1.0, in1=cv, op0=ALU.add, op1=ALU.mult), t1)

        def step_sizes(q):
            pair = slice(2 * q, 2 * q + 2)
            for m_ in (2 * q, 2 * q + 1):
                products = [lambda e, i, b, k=k, m_=m_: e.matmul(
                    b[:, :], w_dt[:, k, m_ * P:(m_ + 1) * P], xb[:, k, :], start=k == 0, stop=k == DK - 1)
                    for k in range(DK)]
                bank, m = fill(products[:DK // 2], last["xb"])
                yield
                m = fill_more(bank, products[DK // 2:])
                yield
                t0 = sc(lambda e, i, m_=m_, bank=bank: e.activation(
                    dtx[:, m_, :], bank[:, :], ACT.Abs, bias=b_dt[:, m_:m_ + 1]), m, last.get(f"drive{q}"))
                t1 = freed(sc(lambda e, i, m_=m_, bank=bank: e.activation(
                    dt[:, m_, :], bank[:, :], ACT.Relu, bias=b_dt[:, m_:m_ + 1]), last.get(f"decay{q}"), last["mod"]),
                    bank)
                t2 = sc(lambda e, i, m_=m_: e.activation(dtx[:, m_, :], dtx[:, m_, :], ACT.Exp, scale=-1.0), t0)
                yield
            if q:
                last["xb_read"] = [m]
            t3 = sc(lambda e, i: e.activation(dtx[:, pair, :], dtx[:, pair, :], ACT.Ln, bias=1.0), t2)
            yield
            last[f"dt{q}"] = ve_(lambda e, i: e.tensor_tensor(
                dt[:, pair, :], dt[:, pair, :], dtx[:, pair, :], ALU.add), t1, t3)
            yield
            last[f"dtx{q}"] = po(lambda e, i: e.tensor_tensor(
                dtx[:, pair, :], dt[:, pair, :], xb[:, pair, :], ALU.mult), last[f"dt{q}"], last["xb"])
            if q:
                last["xb_read"].append(last["dtx1"])
            yield

        def rows_bc():
            bank, m = fill([lambda e, i, b, k=k: e.matmul(
                b[0:SPLIT * BC, :], w_bc[:, k, :], xb[:, k, :], start=k == 0, stop=k == DK - 1)
                for k in range(DK)], last["xb"])
            yield
            last["bc_next"] = yield from split3(bank, m, bc_next, last.get("bc"))
            yield

        def take_bc():
            last["bc"] = sc(lambda e, i: e.activation(bc_stack[:, :], bc_next[:, :], ACT.Copy),
                            last["bc_next"], last.get("bc_read"))
            yield

        def gates():
            for q in range(DK):
                bank, m = fill([lambda e, i, b, k=k, q=q: e.matmul(
                    b[:, :], w_in[:, k, (DK + q) * P:(DK + q + 1) * P], xn_t[:, k, :], start=k == 0, stop=k == HK - 1)
                    for k in range(HK)], last["xn"])
                last["xn_read"] = m
                yield
                t0 = sc(lambda e, i, q=q, bank=bank: e.activation(gz[:, q, :], bank[:, :], ACT.Tanh, scale=0.5),
                        m, last.get("y2_read"))
                yield
                last["gz"] = freed(ve_(lambda e, i, q=q, bank=bank: e.scalar_tensor_tensor(
                    out=gz[:, q, :], in0=gz[:, q, :], scalar=1.0, in1=bank[:, :], op0=ALU.add, op1=ALU.mult), t0), bank)
            yield

        def residual(row):
            ga = pr.dma("sync", "ga", lambda e, i: e.dma_start(
                ga_row[:, :], take(row, i, 2, 3).to_broadcast([P, H])), [last.get("x1"), last["mod"]])
            last["ga"] = ga
            yield
            t = po(lambda e, i: e.tensor_tensor(
                ht[:, :, :], ht[:, :, :], ga_row[:, :].rearrange("p (a h) -> p a h", a=1).to_broadcast(
                    [P, TT, H]), ALU.mult), ga, last["h"], last["normed_h"])
            yield
            last["base"] = po(lambda e, i: e.tensor_tensor(base[:, :, :], xt[:, :, :], ht[:, :, :], ALU.add),
                              t, last.get("x1"))
            yield

        u_done, b_done, c_done, ex_done, scan_done, g_done, add_done, spent = ({} for _ in range(8))

        def broadcast(g, part):
            s = g % BC_RING
            rowi, dst, made, free = ((g % NS, b_bc, b_done, u_done.get(g - BC_RING)),
                                     (NS + g % NS, c_bc, c_done, g_done.get(g - BC_RING)))[part]
            bank, m = fill([lambda e, i, b: e.matmul(
                b[:, :], sel[:, rowi:rowi + 1].to_broadcast([SPLIT * FULL, P]), bc_stack[:, :],
                start=True, stop=True)], last["bc"], last["sel"])
            last["bc_read"] = m
            made[g] = freed(sc(lambda e, i: e.activation(dst[:, s, :], bank[:, :], ACT.Copy), m, free), bank)

        def drive(g):
            q, r, s = g % NU // NS, g % RING, g % BC_RING
            u_done[g] = last[f"drive{q}"] = po(lambda e, i: e.tensor_tensor(
                unit[:, r, :, :], dtx[:, 2 * q:2 * q + 2, :], b_bc[:, s:s + 1, :].to_broadcast([P, 2, T]), ALU.mult),
                b_done[g], last[f"dtx{q}"], spent.get(g - RING))

        def decay(g):
            q, n = g % NU // NS, g % NS
            for a in range(2):
                ex_done[g, a] = last[f"decay{q}"] = sc(lambda e, i, a=a: e.activation(
                    decays[:, a, :], dt[:, 2 * q + a, :], ACT.Exp, scale=a_neg[:, 2 * q + a, n:n + 1]),
                    last[f"dt{q}"], scan_done.get((g - 1, a)))

        def recur(g):
            r = g % RING
            for a in range(2):
                scan_done[g, a] = ve_(lambda e, i, a=a: e.tensor_tensor_scan(
                    unit[:, r, a, :], decays[:, a, :], unit[:, r, a, :], 0.0, ALU.mult, ALU.add),
                    ex_done[g, a], u_done[g])

        def times_c(g):
            r, s = g % RING, g % BC_RING
            g_done[g] = ve_(lambda e, i: e.tensor_tensor(
                unit[:, r, :, :], unit[:, r, :, :], c_bc[:, s:s + 1, :].to_broadcast([P, 2, T]), ALU.mult),
                scan_done[g, 1], c_done[g])

        def add(g, back):
            r0, r1 = (g - back) % RING, g % RING
            add_done[g] = spent[g - back] = po(lambda e, i: e.tensor_tensor(
                unit[:, r1, :, :], unit[:, r1, :, :], unit[:, r0, :, :], ALU.add), g_done[g], add_done.get(g))

        def start_sum(q):
            for a in range(2):
                last["diag_read"] = pe(lambda e, i, a=a: e.matmul(
                    ybank[:, a, :], diag_d[:, 2 * q + a, :], xb[:, 2 * q + a, :], start=True, stop=False),
                    last["xb"], last["diag"], last.get("y_read"))
            if q:
                last["xb_read"].append(last["diag_read"])

        def sum_four(g):
            if g % 4 != 3:
                return
            r = g % RING
            final = g % NS == NS - 1
            for a in range(2):
                spent[g] = last["sums"] = pe(lambda e, i, a=a: e.matmul(
                    ybank[:, a, :], ident[:, :], unit[:, r, a, :], start=False, stop=final), add_done[g])

        def gate_y(g):
            q = g % NU // NS
            for a in range(2):
                last["y2"] = last["y_read"] = ve_(lambda e, i, a=a: e.tensor_tensor(
                    gz[:, 2 * q + a, :], gz[:, 2 * q + a, :], ybank[:, a, :], ALU.mult),
                    last["sums"], last["gz"])

        def beside(k, streams):
            for gen, steps, first, final in streams:
                if first <= k <= final:
                    n = final - first + 1
                    for _ in range((k - first + 1) * steps // n - (k - first) * steps // n):
                        next(gen, None)
                if k == final:
                    left = sum(1 for _ in gen)
                    assert not left, (first, final, steps + left)

        def row_units(index, streams, experts=None, older=None, run=True):
            def half_steps(moment):
                first, final = EXPERTS_AT
                for steps, since in ((older, moment + 3 * NU - first), (experts, moment - first)):
                    while steps and steps.done < steps.HALVES and steps.done * (final - first) < steps.HALVES * since:
                        steps.half_step()

            for k in range(NU if run else 5):
                g = index * NU + k
                if run:
                    recur(g)
                    decay(g + 1)
                if run and k % NS == 5:
                    start_sum(k // NS)
                half_steps(3 * k)
                beside(3 * k, streams)
                if g >= 3 and (run or k < 3) and (g - 3) % 4 == 3:
                    add(g - 3, 2)
                if g >= 1 and (run or k < 1):
                    times_c(g - 1)
                if g >= 2 and (run or k < 2) and g % 2:
                    add(g - 2, 1)
                if k % NS == 4 and g > 4:
                    gate_y(g - 5)
                beside(3 * k + 1, streams)
                half_steps(3 * k + 1)
                if run:
                    broadcast(g + 3, 0)
                    drive(g + 3)
                    broadcast(g + 3, 1)
                if g >= 4 and (run or k < 4):
                    sum_four(g - 4)
                beside(3 * k + 2, streams)
                half_steps(3 * k + 2)

        def first_units():
            for g in range(3):
                broadcast(g, 0)
                drive(g)
                broadcast(g, 1)
            decay(0)

        def project():
            for h in range(2):
                tiles = slice(h * TT // 2, (h + 1) * TT // 2)
                products = [lambda e, i, b, t=t, k=k, h=h: e.matmul(
                    b[:, t * H:(t + 1) * H], gz[:, k, (h * TT // 2 + t) * P:(h * TT // 2 + t + 1) * P], w_out[:, k, :],
                    start=k == 0, stop=k == DK - 1) for t in range(TT // 2) for k in range(DK)]
                bank, m = fill(products[:DK], last["y2"], last["halved"])
                yield
                last["y2_read"] = m = fill_more(bank, products[DK:])
                yield
                t0 = freed(ve_(lambda e, i, bank=bank, tiles=tiles: e.tensor_tensor(
                    x1[:, tiles, :], bank[:, :].rearrange("p (t h) -> p t h", h=H), ga_row[:, :].rearrange(
                        "p (a h) -> p a h", a=1).to_broadcast([P, TT // 2, H]), ALU.mult),
                    m, last["ga"], last.get("moe_add")), bank)
                last["x1"] = ve_(lambda e, i, tiles=tiles: e.tensor_tensor(
                    x1[:, tiles, :], x1[:, tiles, :], base[:, tiles, :], ALU.add), t0, last["base"])

        def load_cols(row):
            last["cols"] = pr.dma("sync", "cols", lambda e, i: e.dma_start(
                mod_col[:, :], take(row, i, 3, 5).rearrange("b (q p) -> p (b q)", p=P)), [last.get("h2")])

        def load_gb(row):
            last["gb"] = pr.dma("sync", "gb", lambda e, i: e.dma_start(
                gb_row[:, :], take(row, i, 5, 6).to_broadcast([P, H])), [last.get("gb_read")])
            yield

        def route(row):
            normed = yield from norm_rows(x1, z2, (st2, mv2, ve2, rstd2), last["x1"], last.get("z2_read"))
            for k in range(HK):
                bank, m = fill([lambda e, i, b, t=t_, k=k: e.transpose(
                    b[:, t * P:(t + 1) * P], z2[:, t, k * P:(k + 1) * P], ident[:, :]) for t_ in range(TT)], normed)
                last["z2_read"] = m
                h2 = freed(sc(lambda e, i, k=k, bank=bank: e.activation(
                    h2_t[:, k, :], bank[:, :], ACT.Identity, bias=mod_col[:, k:k + 1],
                    scale=mod_col[:, HK + k:HK + k + 1]), m, last["cols"], last.get("h2_read")))
                yield
            last["h2"] = h2
            bank, m = fill([lambda e, i, b, t=t_, k=k: e.matmul(
                b[:, t * E:(t + 1) * E], h2_t[:, k, t * P:(t + 1) * P], router_t[:, k, :],
                start=k == 0, stop=k == HK - 1) for t_ in range(TT) for k in range(HK)], h2)
            t = freed(sc(lambda e, i, bank=bank: e.activation(
                r_th[:, :, :].rearrange("p t e -> p (t e)"), bank[:, 0:TT * E], ACT.Tanh, scale=0.5), m))
            yield
            s = ve_(lambda e, i: e.tensor_scalar(r_s[:, :, :], r_th[:, :, :], 0.5, 0.5, ALU.mult, ALU.add), t)
            t = ve_(lambda e, i: e.tensor_tensor(r_ch[:, :, :], r_s[:, :, :], e_bias[:, :].rearrange(
                "p (a e) -> p a e", a=1).to_broadcast([P, TT, E]), ALU.add), s)
            yield
            pairs = r_ch[:, :, :].rearrange("p t (g m) -> p (t g) m", m=GRP)
            hi = ve_(lambda e, i: e.tensor_tensor(r_hi[:, :, :], pairs[:, :, 0:2], pairs[:, :, 2:4], ALU.max), t)
            lo = ve_(lambda e, i: e.tensor_tensor(r_lo[:, :, :], pairs[:, :, 0:2], pairs[:, :, 2:4], ALU.min), t)
            top = ve_(lambda e, i: e.tensor_tensor(r_top[:, :], r_hi[:, :, 0], r_hi[:, :, 1], ALU.max), hi)
            m2 = ve_(lambda e, i: e.tensor_tensor(r_m2[:, :], r_hi[:, :, 0], r_hi[:, :, 1], ALU.min), hi)
            m3 = ve_(lambda e, i: e.tensor_tensor(r_m3[:, :], r_lo[:, :, 0], r_lo[:, :, 1], ALU.max), lo)
            t = ve_(lambda e, i: e.tensor_tensor(r_m2[:, :], r_m2[:, :], r_m3[:, :], ALU.max), m2, m3)
            t = ve_(lambda e, i: e.tensor_tensor(r_g[:, :], r_top[:, :], r_m2[:, :], ALU.add), top, t)
            yield
            g = r_g[:, :].rearrange("p (t g) -> p t g", g=NGRP)
            this = g.rearrange("p t (g a) -> p t g a", a=1).to_broadcast([P, TT, NGRP, NGRP])
            other = g.rearrange("p t (a g) -> p t a g", a=1).to_broadcast([P, TT, NGRP, NGRP])
            low = lower[:, :, :].rearrange("p (a j) i -> p a j i", a=1).to_broadcast([P, TT, NGRP, NGRP])
            gt = ve_(lambda e, i: e.tensor_tensor(r_gt[:, :, :, :], other, this, ALU.is_gt), t)
            t = ve_(lambda e, i: e.tensor_tensor(r_eq[:, :, :, :], other, this, ALU.is_equal), t)
            t = ve_(lambda e, i: e.tensor_tensor(r_eq[:, :, :, :], r_eq[:, :, :, :], low, ALU.mult), t)
            t = ve_(lambda e, i: e.tensor_tensor(r_gt[:, :, :, :], r_gt[:, :, :, :], r_eq[:, :, :, :], ALU.add), t, gt)
            t = ve_(lambda e, i: e.tensor_reduce(r_cnt[:, :], r_gt[:, :, :, :].rearrange("p t j i -> p (t j) i"),
                                                 AX.X, ALU.add), t)
            t = ve_(lambda e, i: e.tensor_scalar(r_msk[:, :], r_cnt[:, :], 1.5, None, ALU.is_lt), t)
            t = ve_(lambda e, i: e.tensor_tensor(
                r_tmp[:, :, 0:E].rearrange("p t (g m) -> p t g m", m=GRP),
                pairs.rearrange("p (t g) m -> p t g m", t=TT),
                r_msk[:, :].rearrange("p (t g a) -> p t g a", t=TT, a=1).to_broadcast([P, TT, NGRP, GRP]),
                ALU.mult), t)
            yield
            pause(t)
            ms = [ve_(lambda e, i, q=q: e.max(r_m8[:, q, :], r_tmp[:, q, 0:E])) for q in range(TT)]
            t8 = ve_(lambda e, i: e.memset(r_m8[:, :, 4:8], NEG), ms[-1])
            pause(t8)
            for q in range(TT):
                t = ve_(lambda e, i, q=q: e.match_replace(r_cut[:, q, :], r_m8[:, q, :], r_tmp[:, q, :], 1.0e38))
            t = ve_(lambda e, i: e.tensor_tensor(r_sel[:, :, :], r_cut[:, :, 0:E], r_tmp[:, :, 0:E], ALU.not_equal), t)
            w = ve_(lambda e, i: e.tensor_tensor(r_w[:, :, :], r_s[:, :, :], r_sel[:, :, :], ALU.mult), t)
            t = ve_(lambda e, i: e.tensor_reduce(r_den[:, :], r_w[:, :, :], AX.X, ALU.add), w)
            t = ve_(lambda e, i: e.tensor_scalar(r_den[:, :], r_den[:, :], 1e-20, 2.0, ALU.add, ALU.mult), t)
            t = ve_(lambda e, i: e.reciprocal(r_rec[:, :], r_den[:, :]), t)
            for s_ in range(SPLIT):
                t3 = ve_(lambda e, i, s_=s_: e.tensor_tensor(
                    w3[:, :, s_ * FULL:s_ * FULL + E], r_w[:, :, :],
                    r_rec[:, :].rearrange("p (t a) -> p t a", a=1).to_broadcast([P, TT, E]), ALU.mult),
                    t, last.get("w3_read"), last["const"])
            yield
            bank, m = fill([lambda e, i, b, t=t_: e.transpose(
                b[0:SPLIT * FULL, t * P:(t + 1) * P], w3[:, t, :], ident[:, :]) for t_ in range(TT)], t3)
            last["w3_read"] = m
            last["w"] = yield from split3(bank, m, w_stack, last.get("w_read"))
            yield

        class Experts:
            HALVES = 2 * (2 * E + 2)

            def __init__(self, row):
                self.row = row
                self.up, self.act, self.w, self.downs, self.bank = {}, {}, {}, {}, {}
                self.done = 0

            def half_step(self):
                s = self.done // 2
                if self.done % 2 == 0:
                    self.gate(s - 1)
                    self.scale(s - 2)
                    self.products(s)
                else:
                    self.weigh(s - 1)
                    self.combine(s - 1)
                    self.down(s - 2)
                self.done += 1

            def ok(self, s):
                return 0 <= s < 2 * E

            def weigh(self, s):
                if not self.ok(s):
                    return
                e_, h = s % E, s // E
                bank, m = fill([lambda e, i, b: e.matmul(
                    b[:, 0:HT], sel[:, e_:e_ + 1].to_broadcast([SPLIT * FULL, P]), w_stack[:, h * HT:(h + 1) * HT],
                    start=True, stop=True)], last["w"])
                last["w_read"] = m
                self.w[s] = freed(sc(lambda e, i: e.activation(w_all[:, s % 2, :], bank[:, 0:HT], ACT.Copy), m,
                                     self.act.get(s - 2) or last.get("act")))

            def products(self, s):
                if not self.ok(s):
                    return
                e_, x = s % E, slice(s // E * HT, (s // E + 1) * HT)
                bank, m = fill([lambda e, i, b, k=k, c=c, w=w: e.matmul(
                    b[:, c * HT:(c + 1) * HT], w[:, e_, k, :], h2_t[:, k, x], start=k == 0, stop=k == HK - 1)
                    for c, w in enumerate((gate_t, up_t)) for k in range(HK)], last["h2"], ring="experts")
                last["h2_read"] = m
                self.bank[s] = (bank, m)

            def gate(self, s):
                if not self.ok(s):
                    return
                bank, m = self.bank[s]
                self.bank[s] += (sc(lambda e, i: e.activation(etanh[:, s % 2, :], bank[:, 0:HT], ACT.Tanh, scale=0.5),
                                    m, last.get(f"etanh{s % 2}")),)

            def combine(self, s):
                if not self.ok(s):
                    return
                bank, m, t0 = self.bank[s]
                a = act[:, s % MOE_RING, :]
                t1 = ve_(lambda e, i: e.scalar_tensor_tensor(
                    out=a, in0=etanh[:, s % 2, :], scalar=1.0, in1=bank[:, 0:HT], op0=ALU.add, op1=ALU.mult),
                    t0, self.downs.get(s - MOE_RING) or last.get("down"))
                last[f"etanh{s % 2}"] = t1
                self.up[s] = freed(ve_(lambda e, i: e.tensor_tensor(a, a, bank[:, HT:2 * HT], ALU.mult), t1), bank)

            def scale(self, s):
                if not self.ok(s):
                    return
                a = act[:, s % MOE_RING, :]
                self.act[s] = ve_(lambda e, i: e.tensor_tensor(a, a, w_all[:, s % 2, :], ALU.mult),
                                  self.up[s], self.w[s])
                last["act"] = self.act[s]

            def down(self, s):
                if not self.ok(s):
                    return
                e_, h = s % E, s // E
                for t in range(TT // 2):
                    last["down"] = self.downs[s] = pe(lambda e, i, t=t: e.matmul(
                        mbank[:, t * H:(t + 1) * H], act[:, s % MOE_RING, t * P:(t + 1) * P], down_t[:, e_, :],
                        start=(e_ == 0 and t == 0), stop=(e_ == E - 1), skip_group_check=True),
                        self.act[s], last.get("moe_read"))
                if e_ == E - 1:
                    self.finish(h)

            def finish(self, h):
                row = self.row
                tiles = slice(h * TT // 2, (h + 1) * TT // 2)
                mo = mbank[:, :].rearrange("p (t h) -> p t h", h=H)
                t0 = ve_(lambda e, i: e.tensor_tensor(z2[:, tiles, :], mo, gb_row[:, :].rearrange(
                    "p (a h) -> p a h", a=1).to_broadcast([P, TT // 2, H]), ALU.mult), last["down"], last["gb"],
                    last["z2_read"], last.get("out"))
                last["moe_read"] = last["gb_read"] = t0
                t0 = po(lambda e, i: e.tensor_tensor(z2[:, tiles, :], z2[:, tiles, :], x1[:, tiles, :], ALU.add), t0)
                last["moe_add"] = t0
                if h == 1:
                    last["out"] = last["z2_read"] = pr.dma("sync", "out", lambda e, i: e.dma_start(
                        out.rearrange("b (t p) h -> p b t h", p=P)[:, bass.ds(row(i), 1), :, :].rearrange(
                            "p b t h -> p (b t) h"), z2[:, :, :]), [t0])

        def chain(*streams):
            for s in streams:
                yield from s

        pr.begin()
        setup()
        for _ in chain(prepare(lambda i: 0), silu_inputs(), rows_bc(), take_bc(), step_sizes(0)):
            pass
        first_units()

        def around(row, coming, behind=None):
            streams = []
            if behind is not None:
                load_cols(behind)
                streams = [(load_gb(behind), 1, 16, 16), (project(), 4, 13, 17), (route(behind), 15, 18, 31)]
            return streams + [
                (residual(row), 4, 18, 23), (step_sizes(1), 9, 30, 37), (gates(), 9, 25, 30),
                (prepare(coming), 13, 25, 39), (silu_inputs(), 12, 62, 70), (rows_bc(), 5, 82, 85),
                (step_sizes(0), 9, 74, 82), (take_bc(), 2, 88, 88)]

        row_units(0, around(lambda i: 0, lambda i: 1))
        def later_row(index, this, older):
            assert "held" not in [work["free"][k] for k in rings["work"]]
            rings["work"] = [0, 1, 2]
            if older:
                older.row = lambda i: this(i) - 2
            experts = Experts(lambda i: this(i) - 1)
            row_units(index, around(this, lambda i: (this(i) + 1) % NB, lambda i: this(i) - 1), experts, older)
            return experts

        pr.begin()
        running = later_row(1, lambda i: 1, None)
        pr.begin()
        running = later_row(2, lambda i: 2, running)
        pr.begin(loop=(3, NB))
        running = later_row(3, lambda i: i, running)
        pr.begin()
        running.row = lambda i: NB - 2
        row_units(4, [], older=running, run=False)
        load_cols(lambda i: NB - 1)
        for _ in chain(load_gb(lambda i: NB - 1), project(), route(lambda i: NB - 1)):
            pass
        last_row = Experts(lambda i: NB - 1)
        while last_row.done < last_row.HALVES:
            last_row.half_step()
        pr.close()

        ctx.enter_context(nc.allow_non_contiguous_dma(reason="small vectors onto partitions"))
        block = ctx.enter_context(nc.Block())

        @block.tensor
        def _(eng):
            pr.replay(eng, "tensor")

        @block.vector
        def _(eng):
            pr.replay(eng, "vector")

        @block.scalar
        def _(eng):
            pr.replay(eng, "scalar")

        @block.gpsimd
        def _(eng):
            pr.replay(eng, "gpsimd")

        @block.sync
        def _(eng):
            pr.replay(eng, "sync")
            eng.wait_ge(dma_sems["out"], pr.totals[dma_sems["out"]])


_INS = ['L0_attn_x', 'L0_attn_norm_scale', 'L0_attn_norm_bias', 'L0_attn_W_in', 'L0_attn_conv_w', 'L0_attn_conv_b',
        'L0_attn_W_dt', 'L0_attn_b_dt', 'L0_attn_A_log', 'L0_attn_D_param', 'L0_attn_W_B', 'L0_attn_W_C',
        'L0_attn_W_out', 'L0_ffn_gate_weight', 'L0_ffn_e_bias', 'L0_ffn_gate_proj', 'L0_ffn_up_proj',
        'L0_ffn_down_proj', 'L0_c', 'L0_wmod']


def kernel(**inputs):
    import numpy as _np
    import concourse.bacc as _bacc
    from concourse import mybir as _mybir
    from concourse.bass_utils import run_bass_kernel_spmd as _run

    nc = _bacc.Bacc("TRN2", target_bir_lowering=False, num_devices=1)
    arrays, aps = {}, {}
    for name in _INS:
        a = _np.ascontiguousarray(inputs[name])
        arrays[f"in_{name}_dram"] = a
        aps[name] = nc.dram_tensor(f"in_{name}_dram", a.shape, _mybir.dt.from_np(a.dtype), kind="ExternalInput").ap()
    shape = inputs["L0_attn_x"].shape
    out = nc.dram_tensor("out_0_dram", shape, _mybir.dt.float32, kind="ExternalOutput").ap()
    build(nc, aps, out)
    r = _run(nc, [arrays], core_ids=[0])
    return r.results[0]["out_0_dram"]
```
